# Optimizing a Trainium2 kernel written in Bass

```python
import numpy as np
import jax
import jax.numpy as jnp

def _softmax(x, axis=-1):
    return jax.nn.softmax(x, axis=axis)

def _gelu(x):
    return jax.nn.gelu(x, approximate=True)

def _silu(x):
    return jax.nn.silu(x)

def _sigmoid(x):
    return jax.nn.sigmoid(x)

def _layernorm(x, axis=-1, eps=1e-05):
    m = jnp.mean(x, axis=axis, keepdims=True)
    v = jnp.var(x, axis=axis, keepdims=True)
    return (x - m) / jnp.sqrt(v + eps)

def _scatter_add(tgt, idx, src, axis=0):
    return tgt.at[idx].add(src)

def _segment_sum(src, seg, n):
    return jax.ops.segment_sum(src, seg, n)
kernel_name = 'mk_adj_resnorm_d2_adj_r2_a21315'

def setup_inputs(seed: int=0):
    np.random.seed(seed)
    _w = jnp.asarray

    def _rec_inputs():
        import jax
        import jax.numpy as jnp
        _gk = jax.random.key(seed)
        x = -0.000929 + 1 * jax.random.normal(jax.random.fold_in(_gk, 1), (4096, 128), jnp.float32)
        _a = jax.random.bernoulli(jax.random.fold_in(_gk, 2), 0.000976562, (4096, 4096))
        _af = _a.astype(jnp.float32)
        adj = _af
        return (x, adj)
    x, adj = _rec_inputs()

    def _L0_gnn_setup():
        import jax, jax.numpy as jnp
        import numpy as np
        N, D = (4096, 128)
        EDGE_PROB = 0.005
        COS_EPS = 1e-08
        key = jax.random.key(seed)
        kx, ka = jax.random.split(key)
        x = jax.random.normal(kx, (N, D), dtype=jnp.float32)
        adj = (jax.random.uniform(ka, (N, N)) < EDGE_PROB).astype(jnp.float32)
        return {'t': jnp.float32(0.0), 'x': x, 'adj': adj, 'alpha': jnp.float32(0.5), 'beta': jnp.float32(1.0)}
    _L0_gnn_all = _L0_gnn_setup()
    _L0_gnn_in = {k: v for k, v in _L0_gnn_all.items() if k in ('t', 'alpha', 'beta')}
    del _L0_gnn_all

    def _L1_gnn_setup():
        import jax, jax.numpy as jnp
        import numpy as np
        N = 8192
        IN_DIM = 128
        OUT_DIM = 128
        key = jax.random.key(seed)
        k1, k2, k3 = jax.random.split(key, 3)
        X = jax.random.normal(k1, (N, IN_DIM), dtype=jnp.float32)
        adjm = jax.random.uniform(k2, (N, N), dtype=jnp.float32)
        stdv = float(np.sqrt(2.0 / (IN_DIM + OUT_DIM)))
        weights = jax.random.uniform(k3, (IN_DIM, OUT_DIM), dtype=jnp.float32, minval=-stdv, maxval=stdv)
        return {'X': X, 'adjm': adjm, 'weights': weights}
    _L1_gnn_all = _L1_gnn_setup()
    _L1_gnn_in = {k: v for k, v in _L1_gnn_all.items() if k in ('weights',)}
    del _L1_gnn_all
    return {'x': x, 'adj': adj, 'L0_gnn_t': _L0_gnn_in['t'], 'L0_gnn_alpha': _L0_gnn_in['alpha'], 'L0_gnn_beta': _L0_gnn_in['beta'], 'L1_gnn_weights': _L1_gnn_in['weights']}

def reference(x, adj, L0_gnn_t, L0_gnn_alpha, L0_gnn_beta, L1_gnn_weights):
    import jax
    import jax.numpy as jnp

    def _L0_gnn_ref(t, x, adj, alpha, beta):
        import jax, jax.numpy as jnp
        import numpy as np
        N, D = (4096, 128)
        EDGE_PROB = 0.005
        COS_EPS = 1e-08
        deg = jnp.clip(adj.sum(axis=1), 1.0)
        dis = deg ** (-0.5)
        adj_norm = dis[:, None] * adj * dis[None, :]
        diffusion = adj_norm @ x - x
        norms = jnp.maximum(jnp.linalg.norm(x, axis=-1), COS_EPS)
        sim = x @ x.T / (norms[:, None] * norms[None, :])
        attn = jax.nn.softmax(beta * sim * adj, axis=1)
        attn = jax.lax.stop_gradient(attn)
        return diffusion + jax.nn.sigmoid(alpha) * (attn @ x - x)

    def _L1_gnn_ref(X, adjm, weights):
        import jax, jax.numpy as jnp
        import numpy as np
        N = 8192
        IN_DIM = 128
        OUT_DIM = 128
        XW = jnp.matmul(X, weights)
        Y = jnp.matmul(adjm, XW)
        return jax.nn.relu(Y)
    x = _layernorm(x + _L0_gnn_ref(L0_gnn_t, x, adj, L0_gnn_alpha, L0_gnn_beta), axis=-1)
    x = _layernorm(x + _L1_gnn_ref(x, adj, L1_gnn_weights), axis=-1)
    return x

_drawn_inputs = setup_inputs


def setup_inputs(seed=0):
    import zlib

    import numpy as np

    out = dict(_drawn_inputs(seed))
    spreads = {}
    factors = {}
    for name, (base, spread) in spreads.items():
        noise = np.random.default_rng([zlib.crc32(name.encode()), seed]).standard_normal(out[name].shape)
        drawn = base * np.exp(spread * noise) if base else spread * noise
        out[name] = jnp.asarray(drawn.astype(out[name].dtype))
    for name, factor in factors.items():
        out[name] = (out[name] * factor).astype(out[name].dtype)
    return out
```

```python
from contextlib import ExitStack

import concourse.bass as bass
from concourse import mybir

ALU = mybir.AluOpType
ACT = mybir.ActivationFunctionType
AX = mybir.AxisListType
F32 = mybir.dt.float32
F16 = mybir.dt.float16
F8 = mybir.dt.float8e4
U8 = mybir.dt.uint8
U32 = mybir.dt.uint32
I32 = mybir.dt.int32

P = 128
K = 4
BANK = 512
BYTE_ONE = 64.0
BYTE_F8 = 2.0
XN_SCALE = 64.0
E_SCALE = 4096.0
X_SCALE = 4096.0
W_SCALE = 128.0
LN_EPS = 1e-5
MIN_NORM = 1e-8
LOWEST = -3.0e38


def two_layer_gnn(nc, x, adj, alpha, beta, weights, out):
    N, D = x.shape
    R = N // P
    B = R // K
    CH = 1024
    C = N // CH
    TC = CH // P
    H = N // BANK
    TH = BANK // P
    LAND = N // 2
    G = 4
    assert D == P and C == 4 and H == 8 and R == 32 and B == 8

    with ExitStack() as ctx:
        def sb(name, shape, dt):
            return ctx.enter_context(nc.sbuf_tensor(name, shape, dt))

        def psum(name, shape, dt):
            return ctx.enter_context(nc.psum_tensor(name, shape, dt))

        def sem(name):
            return ctx.enter_context(nc.semaphore(name))

        adjT = sb("adjT", [P, R, B, P], U32)
        land = sb("land", [P, 2, LAND], F32)
        adj_bytes = sb("adj_bytes", [P, 2, N], U8)
        x_parts = sb("x_parts", [P, R, 2 * D], F16)
        xn_parts = sb("xn_parts", [P, 2, N], F16)
        xn_signed = sb("xn_signed", [P, 2, 2, P], F16)
        scores = sb("scores", [P, N], F32)
        u = sb("u", [P, R, D], F32)
        eT_parts = sb("eT_parts", [P, 2, 2, BANK], F16)
        ident = sb("ident", [P, P], F32)
        col = sb("col", [P, 26], F32)
        norm = sb("norm", [P, R], F32)
        deg = sb("deg", [P, 2, R], F32)
        dis = sb("dis", [P, R], F32)
        dis_out = sb("dis_out", [P, R], F32)
        cmax = sb("cmax", [P, H], F32)
        csum = sb("csum", [P, C], F32)
        stats = sb("stats", [P, 6], F32)
        mv = sb("mv", [P, 2, 2], F32)

        def c(n):
            return col[:, n:n + 1]
        alpha_c, beta_c, e_alpha, sigma, neg_sigma, abs_beta = (c(n) for n in range(6))
        neg_max, total, r_total, gain = (c(n) for n in range(6, 10))
        attn_scale, x_up, dif_scale, w_up, w_down, eps_c = (c(n) for n in range(10, 16))
        great = col[:, 16:18]
        pow2 = col[:, 18:20]
        rpow2 = col[:, 20:22]
        std = col[:, 22:24]
        sign_beta, top = c(24), c(25)
        rstd = sb("rstd", [P, 2], F32)

        ps_s = psum("ps_s", [P, 4, BANK], F32)
        ps_e = psum("ps_e", [P, 2, BANK], F32)
        ps_acc = psum("ps_acc", [P, BANK], F32)
        ps_at = psum("ps_at", [P, BANK], F32)

        x_loaded = [sem(f"x_loaded{q}") for q in range(C)]
        small_loaded = sem("small_loaded")
        w_loaded = sem("w_loaded")
        land_full = [sem("land_full0"), sem("land_full1")]
        x_again = sem("x_again")
        ident_zero = sem("ident_zero")
        ident_done = sem("ident_done")
        squares_done = sem("squares_done")
        norms2_done = sem("norms2_done")
        root_done = sem("root_done")
        dve_step = sem("dve_step")
        xn_done = sem("xn_done")
        xnt_turned = sem("xnt_turned")
        xnt_hi = sem("xnt_hi")
        xnt_lo = sem("xnt_lo")
        sign_done = sem("sign_done")
        signed = sem("signed")
        top_done = sem("top_done")
        great_done = sem("great_done")
        great_turned = sem("great_turned")
        great_diag = sem("great_diag")
        great_spread = sem("great_spread")
        scales_done = sem("scales_done")
        alpha_exp = sem("alpha_exp")
        sigma_done = sem("sigma_done")
        x_hi = sem("x_hi")
        x_lo = sem("x_lo")
        u_init = sem("u_init")
        cast_done = [sem("cast_done0"), sem("cast_done1")]
        adj_turned = sem("adj_turned")
        adj_stored = sem("adj_stored")
        s_done = sem("s_done")
        scores_done = sem("scores_done")
        max_done = sem("max_done")
        exp_done = sem("exp_done")
        e_turned = sem("e_turned")
        e_hi = sem("e_hi")
        e_lo = sem("e_lo")
        attn_part = sem("attn_part")
        u_half = sem("u_half")
        attn_read = sem("attn_read")
        total_done = sem("total_done")
        deg_done = sem("deg_done")
        deg_root = sem("deg_root")
        dis_done = sem("dis_done")
        y_done = sem("y_done")
        y_hi = sem("y_hi")
        y_lo = sem("y_lo")
        staged = sem("staged")
        rows_done = sem("rows_done")
        sums_read = sem("sums_read")
        hi_added = sem("hi_added")
        bn_done = sem("bn_done")
        var_done = sem("var_done")
        std_done = sem("std_done")
        rstd_done = sem("rstd_done")
        x1_done = sem("x1_done")
        x1_turned = sem("x1_turned")
        x1_kept = sem("x1_kept")
        out_done = sem("out_done")
        x1t_done = sem("x1t_done")
        xw_done = sem("xw_done")
        xw_hi = sem("xw_hi")
        xw_lo = sem("xw_lo")
        relu_done = sem("relu_done")
        out_stored = sem("out_stored")

        x_v = x.rearrange("(b p k) d -> p b (k d)", p=P, k=K)
        out_v = out.rearrange("(b p k) d -> b p (k d)", p=P, k=K)
        adj_v = adj.rearrange("(b p k) j -> b k p j", p=P, k=K)
        u_b = u[:, :, :].rearrange("p (b k) d -> p b (k d)", k=K)
        x2 = land[:, :, :].rearrange("p h (r d) -> p (h r) d", d=D)
        y_parts = xn_parts[:, :, :].rearrange("p a (r d) -> p (a r) d", d=2 * D)
        x1t = scores[:, 0:2 * P].rearrange("p (a d) -> p a d", d=P)
        x1_now = scores[:, 2 * P:4 * P].rearrange("p (a d) -> p a d", d=P)
        wts = scores[:, 4 * P:5 * P]
        summed = scores[:, 5 * P:6 * P]
        xw_ps = [ps_acc, ps_at]
        wts_early = eT_parts[:, 0, 0, 0:2 * P].bitcast(F32)
        ones2 = eT_parts[0:2, 1, 1, 0:2 * P].bitcast(F32)
        mean = [mv[:, q, 0:1] for q in range(2)]
        var = [mv[:, q, 1:2] for q in range(2)]
        words = [adj_bytes[:, q, :].bitcast(F32) for q in range(2)]
        stage = [adj_bytes[:, q, :].bitcast(U32) for q in range(2)]
        stage8 = [adj_bytes[:, q, :].bitcast(F8).rearrange("p (b i k) -> p b i k", b=B, k=K) for q in range(2)]
        adjT8 = [adjT[:, r, :, :].rearrange("p b i -> p (b i)").bitcast(F8)
                 .rearrange("p (b i k) -> p b i k", b=B, k=K) for r in range(G)]
        adjT_rows = adjT[:, :, :, :].rearrange("p r b i -> p r (b i)")

        block = ctx.enter_context(nc.Block())

        @block.sync
        def _(sp):
            for q in range(C):
                sp.dma_start(u_b[:, 2 * q:2 * q + 2, :], x_v[:, 2 * q:2 * q + 2, :]).then_inc(x_loaded[q], 16)
            sp.dma_start(alpha_c, alpha.rearrange("(a o) -> a o", o=1).to_broadcast([P, 1])).then_inc(small_loaded, 16)
            sp.dma_start(beta_c, beta.rearrange("(a o) -> a o", o=1).to_broadcast([P, 1])).then_inc(small_loaded, 16)
            sp.dma_start(wts_early, weights).then_inc(w_loaded, 16)
            for h in range(2):
                sp.dma_start(land[:, h, :], adj_v[0, 0, :, h * LAND:(h + 1) * LAND]).then_inc(land_full[h], 16)
            for k in range(1, K):
                for h in range(2):
                    sp.wait_ge(cast_done[h], k)
                    sp.dma_start(land[:, h, :], adj_v[0, k, :, h * LAND:(h + 1) * LAND]).then_inc(land_full[h], 16)
            with sp.Fori(1, B) as b:
                for k in range(K):
                    for h in range(2):
                        sp.wait_ge(cast_done[h], b * K + k)
                        sp.dma_start(land[:, h, :], adj_v[b, k, :, h * LAND:(h + 1) * LAND]).then_inc(land_full[h], 16)
            sp.wait_ge(e_turned, R * H)
            sp.dma_start(wts, weights).then_inc(w_loaded, 16)
            for h in range(2):
                sp.wait_ge(cast_done[h], R)
                sp.dma_start(land[:, h, :].rearrange("p (b x) -> p b x", b=B // 2),
                             x_v[:, h * B // 2:(h + 1) * B // 2, :]).then_inc(x_again, 16)
            with sp.Fori(0, B) as b:
                sp.wait_ge(out_done, b * K + K)
                sp.dma_start(out_v[b], u_b[:, b, :]).then_inc(out_stored, 16)
            sp.wait_ge(out_stored, 16 * B)

        @block.gpsimd
        def _(pool):
            nc.gpsimd.memset(ones2, 1.0)
            nc.gpsimd.memset(ident[:, :], 0.0).then_inc(ident_zero, 1)
            pool.wait_ge(ident_zero, 1)
            nc.gpsimd.affine_select(out=ident[:, :], in_=ident[:, :], compare_op=ALU.not_equal, fill=1.0, base=0,
                                    pattern=[[-1, P]], channel_multiplier=1).then_inc(ident_done, 1)

            def sign_block(r, q, first=False):
                if not first:
                    pool.wait_ge(s_done, r * C - C)
                nc.gpsimd.tensor_tensor(xn_signed[:, q, :, :], xn_parts[:, :, bass.ds(r * P, P)],
                                        sign_beta.unsqueeze(2).to_broadcast([P, 2, P]), ALU.mult).then_inc(signed, 1)

            pool.wait_ge(sign_done, 1)
            pool.wait_ge(xnt_lo, 1)
            sign_block(0, 0, first=True)
            sign_block(1, 1, first=True)
            pool.wait_ge(sigma_done, 1)
            for q in range(C):
                pool.wait_ge(xn_done, q + 1)
                pool.wait_ge(x_lo, q + 1)
                v = u[:, q * TC:(q + 1) * TC, :].rearrange("p r d -> p (r d)")
                nc.gpsimd.tensor_scalar(v, v, neg_sigma, 1.0, ALU.mult, ALU.mult).then_inc(u_init, 1)

            with pool.Fori(2, R - 1, 2) as r:
                sign_block(r, 0)
                sign_block(r + 1, 1)

            for layer in range(2):
                base = layer * R
                if layer == 0:
                    pool.wait_ge(scores_done, C * R)
                    pool.wait_ge(adj_stored, 2 * R)
                else:
                    pool.wait_ge(rows_done, R - 1)
                for q in range(2):
                    if layer == 1 and q == 1:
                        pool.wait_ge(rows_done, R)
                    nc.gpsimd.tensor_copy(stage[q], adjT_rows[:, G + q, :]).then_inc(staged, 1)
                with pool.Fori(G + 2, R - 1, 2) as r:
                    for q in range(2):
                        pool.wait_ge(rows_done, r + (base + q - 1))
                        nc.gpsimd.tensor_copy(stage[q], adjT_rows[:, r + q, :]).then_inc(staged, 1)

        @block.scalar
        def _(act):
            act.wait_ge(small_loaded, 32)
            nc.scalar.activation(e_alpha, alpha_c, ACT.Exp, scale=-1.0).then_inc(alpha_exp, 1)
            for q in range(C):
                act.wait_ge(x_loaded[q], 16)
                nc.scalar.activation(scores[:, q * CH:(q + 1) * CH],
                                     u[:, q * TC:(q + 1) * TC, :].rearrange("p r d -> p (r d)"),
                                     ACT.Square).then_inc(squares_done, 1)
            act.wait_ge(norms2_done, 1)
            nc.scalar.activation(norm[:, :], norm[:, :], ACT.Sqrt).then_inc(root_done, 1)

            def cast(r, q, h):
                act.wait_ge(land_full[h], 16 * r + 16)
                nc.scalar.activation(adj_bytes[:, q, h * LAND:(h + 1) * LAND], land[:, h, :], ACT.Copy,
                                     scale=BYTE_ONE, accum_out=deg[:, h, bass.ds(r, 1)]).then_inc(cast_done[h], 1)

            def xnt_high(g):
                act.wait_ge(xnt_turned, g + 1)
                nc.scalar.activation(xn_parts[:, 0, g * BANK:(g + 1) * BANK], ps_e[:, g % 2, :],
                                     ACT.Copy).then_inc(xnt_hi, 1)

            for g in range(H):
                xnt_high(g)
                if g == 3:
                    cast(0, 0, 0)
                if g == 5:
                    cast(0, 0, 1)
            act.wait_ge(scales_done, 1)
            for q in range(C):
                nc.scalar.activation(x_parts[:, q * TC:(q + 1) * TC, 0:D], u[:, q * TC:(q + 1) * TC, :],
                                     ACT.Copy, scale=x_up).then_inc(x_hi, 1)
            for h in range(2):
                cast(1, 1, h)

            def exps(r, i):
                if i == 0:
                    act.wait_ge(max_done, r + 1)
                nc.scalar.activation(scores[:, i * CH:(i + 1) * CH], scores[:, i * CH:(i + 1) * CH], ACT.Exp,
                                     bias=neg_max, scale=abs_beta, accum_out=csum[:, i:i + 1]).then_inc(exp_done, 1)

            def e_high(r, h, start):
                act.wait_ge(e_turned, r * H + (h + 1))
                if not (start and h < 2):
                    act.wait_ge(attn_part, r * H + (h - 1))
                nc.scalar.activation(eT_parts[:, h % 2, 0, :], ps_e[:, h % 2, :], ACT.Copy,
                                     scale=E_SCALE).then_inc(e_hi, 1)

            def row(r, q, start=False, last=False):
                exps(r, 0)
                exps(r, 1)
                for h in range(H):
                    e_high(r, h, start)
                    if h == 1:
                        exps(r, 2)
                    if h == 3:
                        exps(r, 3)
                if not last:
                    for h in range(2):
                        cast(r + 2, q, h)

            row(0, 0, start=True)
            row(1, 1)
            with act.Fori(2, R - 3, 2) as r:
                row(r, 0)
                row(r + 1, 1)
            row(R - 2, 0, last=True)
            row(R - 1, 1, last=True)

            act.wait_ge(deg_done, 1)
            nc.scalar.activation(dis[:, :], dis[:, :], ACT.Sqrt).then_inc(deg_root, 1)
            for q in range(C):
                act.wait_ge(y_done, q + 1)
                nc.scalar.activation(y_parts[:, q * TC:(q + 1) * TC, 0:D], x2[:, q * TC:(q + 1) * TC, :],
                                     ACT.Copy).then_inc(y_hi, 1)

            def root(r, q, base):
                act.wait_ge(var_done, r + (base + 1))
                nc.scalar.activation(std[:, q:q + 1], var[q], ACT.Sqrt, bias=eps_c).then_inc(std_done, 1)

            def turned_out(r, q):
                act.wait_ge(x1_done, r + 1)
                nc.scalar.activation(u[:, r, :], x1_now[:, q, :], ACT.Copy).then_inc(x1_kept, 1)
                act.wait_ge(x1_turned, r + 1)
                nc.scalar.activation(x1t[:, q, :], ps_e[:, q, 0:P], ACT.Copy).then_inc(x1t_done, 1)

            def xw_high(r, q):
                act.wait_ge(xw_done, r + 1)
                nc.scalar.activation(x_parts[:, r, 0:D], xw_ps[q][:, 0:P], ACT.Copy,
                                     scale=w_up).then_inc(xw_hi, 1)

            def step(r, q, lag):
                root(r, q, 0)
                if lag >= 2:
                    turned_out(r - 2, q)
                if lag >= 3:
                    xw_high(r - 3, 1 - q)
            for r in range(4):
                step(r, r % 2, r)
            with act.Fori(4, R - 1, 2) as r:
                step(r, 0, 3)
                step(r + 1, 1, 3)
            turned_out(R - 2, 0)
            xw_high(R - 3, 1)
            turned_out(R - 1, 1)
            xw_high(R - 2, 0)
            xw_high(R - 1, 1)
            with act.Fori(0, R - 1, 2) as r:
                root(r, 0, R)
                root(r + 1, 1, R)

        @block.vector
        def _(dve):
            steps = [0]

            def link(ins):
                steps[0] += 1
                ins.then_inc(dve_step, 1)
                dve.wait_ge(dve_step, steps[0])

            link(nc.vector.memset(eps_c, LN_EPS))
            dve.wait_ge(small_loaded, 32)
            link(nc.vector.tensor_scalar(sign_beta, beta_c, 0.0, 2.0, ALU.is_ge, ALU.mult))
            link(nc.vector.tensor_scalar(sign_beta, sign_beta, -1.0, None, ALU.add))
            nc.vector.tensor_scalar(abs_beta, beta_c, sign_beta, None, ALU.mult).then_inc(sign_done, 1)
            for q in range(C):
                dve.wait_ge(squares_done, q + 1)
                last = nc.vector.tensor_reduce(norm[:, q * TC:(q + 1) * TC],
                                               scores[:, q * CH:(q + 1) * CH].rearrange("p (r d) -> p r d", d=D),
                                               AX.X, ALU.add)
            link(last)
            nc.vector.tensor_scalar(norm[:, :], norm[:, :], MIN_NORM * MIN_NORM, None, ALU.max).then_inc(norms2_done, 1)
            dve.wait_ge(root_done, 1)
            link(nc.vector.reciprocal(dis[:, :], norm[:, :]))
            link(nc.vector.tensor_scalar(dis[:, :], dis[:, :], XN_SCALE, None, ALU.mult))
            for q in range(C):
                nc.vector.tensor_tensor(
                    scores[:, q * CH:(q + 1) * CH].rearrange("p (r d) -> p r d", d=D),
                    u[:, q * TC:(q + 1) * TC, :],
                    dis[:, q * TC:(q + 1) * TC].unsqueeze(2).to_broadcast([P, TC, D]), ALU.mult).then_inc(xn_done, 1)
            dve.wait_ge(w_loaded, 16)
            link(nc.vector.tensor_reduce(great[:, 1:2], wts_early, AX.X, ALU.max, apply_absolute_value=True))
            nc.vector.tensor_reduce(great[:, 0:1], norm[:, :], AX.X, ALU.max).then_inc(great_done, 1)

            def xnt_low(g):
                dve.wait_ge(xnt_hi, g + 1)
                nc.vector.tensor_tensor(xn_parts[:, 1, g * BANK:(g + 1) * BANK], ps_e[:, g % 2, :],
                                        xn_parts[:, 0, g * BANK:(g + 1) * BANK], ALU.subtract).then_inc(xnt_lo, 1)

            xnt_low(0)
            xnt_low(1)
            dve.wait_ge(great_turned, 1)
            link(nc.vector.tensor_reduce(top[0:2, :], ps_at[0:2, 0:P], AX.X, ALU.max))
            nc.vector.tensor_scalar(pow2[0:2, :], ident[0:2, 0:2], top[0:2, :], None,
                                    ALU.mult).then_inc(great_diag, 1)
            xnt_low(2)
            xnt_low(3)
            dve.wait_ge(great_spread, 1)
            link(nc.vector.tensor_scalar(pow2, ps_at[:, 2 * P:2 * P + 2], 1e-30, 1e30, ALU.max, ALU.min))
            link(nc.vector.tensor_scalar(pow2.bitcast(I32), pow2.bitcast(I32), 0x7F800000, None, ALU.bitwise_and))
            link(nc.vector.reciprocal(rpow2, pow2))
            dve.wait_ge(alpha_exp, 1)
            link(nc.vector.tensor_scalar(sigma, e_alpha, 1.0, None, ALU.add))
            link(nc.vector.reciprocal(sigma, sigma))
            nc.vector.tensor_scalar(neg_sigma, sigma, -1.0, None, ALU.mult).then_inc(sigma_done, 1)
            link(nc.vector.tensor_scalar(w_up, rpow2[:, 1:2], W_SCALE, None, ALU.mult))
            link(nc.vector.tensor_scalar(w_down, pow2[:, 1:2], 1.0 / (W_SCALE * BYTE_F8), None, ALU.mult))
            link(nc.vector.tensor_scalar(dif_scale, pow2[:, 0:1], 1.0 / (X_SCALE * BYTE_F8), None, ALU.mult))
            link(nc.vector.tensor_scalar(attn_scale, pow2[:, 0:1], sigma, 1.0 / (X_SCALE * E_SCALE), ALU.mult, ALU.mult))
            nc.vector.tensor_scalar(x_up, rpow2[:, 0:1], X_SCALE, None, ALU.mult).then_inc(scales_done, 1)
            dve.wait_ge(scales_done, 1)
            for g in range(4, H):
                xnt_low(g)

            def store_adj(r, g):
                dve.wait_ge(adj_turned, 2 * r + (g + 1))
                nc.vector.tensor_copy(adjT_rows[:, r, g * BANK:(g + 1) * BANK],
                                      ps_at[:, :].bitcast(U32)).then_inc(adj_stored, 1)

            def mask(r, q, i, start=False):
                dve.wait_ge(s_done, r * C + (i + 1))
                if not start:
                    dve.wait_ge(e_turned, r * H + (2 * i + 2 - H))
                dve.wait_ge(cast_done[i // 2], r + 1)
                for n in range(2):
                    ins = nc.vector.tensor_tensor_reduce(
                        scores[:, i * CH + n * BANK:i * CH + (n + 1) * BANK].rearrange("p (k q) -> p k q", k=K),
                        ps_s[:, 2 * (i % 2) + n, :].rearrange("p (k q) -> p k q", k=K),
                        adj_bytes[:, q, i * CH + n * BANK:i * CH + (n + 1) * BANK].rearrange("p (q k) -> p k q", k=K),
                        1.0 / (XN_SCALE * XN_SCALE * BYTE_ONE), LOWEST, ALU.mult, ALU.max, cmax[:, 2 * i + n:2 * i + n + 1])
                    if n == 0:
                        ins.wait_op(sign_done, 1, "sem-ge")
                ins.then_inc(scores_done, 1)

            def row_max(r):
                dve.wait_ge(scores_done, r * C + C)
                nc.vector.tensor_reduce(top, cmax[:, :], AX.X, ALU.max, negate=True).then_inc(top_done, 1)
                dve.wait_ge(top_done, r + 1)
                nc.vector.tensor_scalar(neg_max, top, abs_beta, None, ALU.mult).then_inc(max_done, 1)

            def e_low(r, h):
                dve.wait_ge(e_hi, r * H + (h + 1))
                nc.vector.scalar_tensor_tensor(eT_parts[:, h % 2, 1, :], ps_e[:, h % 2, :], E_SCALE,
                                               eT_parts[:, h % 2, 0, :], ALU.mult, ALU.subtract).then_inc(e_lo, 1)

            def attn_add(r):
                dve.wait_ge(attn_part, r * H + H)
                dve.wait_ge(total_done, 3 * r + 3)
                nc.vector.scalar_tensor_tensor(u[:, r, :], ps_acc[:, 0:D], gain, u[:, r, :],
                                               ALU.mult, ALU.add).then_inc(u_half, 1)
                dve.wait_ge(u_half, r + 1)
                nc.vector.scalar_tensor_tensor(u[:, r, :], ps_acc[:, D:2 * D], gain, u[:, r, :],
                                               ALU.mult, ALU.add).then_inc(attn_read, 1)

            def total_step(r, n):
                if n == 0:
                    dve.wait_ge(exp_done, r * C + C)
                    ins = nc.vector.tensor_reduce(total, csum[:, :], AX.X, ALU.add)
                elif n == 1:
                    dve.wait_ge(total_done, 3 * r + 1)
                    ins = nc.vector.reciprocal(r_total, total)
                else:
                    dve.wait_ge(total_done, 3 * r + 2)
                    ins = nc.vector.tensor_scalar(gain, r_total, attn_scale, None, ALU.mult)
                ins.then_inc(total_done, 1)

            for g in range(2):
                store_adj(0, g)
            for i in range(C):
                mask(0, 0, i, start=True)
            row_max(0)
            for q in range(C):
                dve.wait_ge(x_hi, q + 1)
                nc.vector.scalar_tensor_tensor(x_parts[:, q * TC:(q + 1) * TC, D:2 * D],
                                               u[:, q * TC:(q + 1) * TC, :], x_up,
                                               x_parts[:, q * TC:(q + 1) * TC, 0:D],
                                               ALU.mult, ALU.subtract).then_inc(x_lo, 1)

            def row(r, q, start=False, last=False):
                if not last:
                    store_adj(r + 1, 0)
                if not start:
                    attn_add(r - 1)
                if not last:
                    store_adj(r + 1, 1)
                e_low(r, 0)
                if not last:
                    mask(r + 1, 1 - q, 0)
                e_low(r, 1)
                e_low(r, 2)
                if not last:
                    mask(r + 1, 1 - q, 1)
                e_low(r, 3)
                e_low(r, 4)
                if not last:
                    mask(r + 1, 1 - q, 2)
                e_low(r, 5)
                total_step(r, 0)
                e_low(r, 6)
                total_step(r, 1)
                e_low(r, 7)
                total_step(r, 2)
                if not last:
                    mask(r + 1, 1 - q, 3)
                    row_max(r + 1)

            row(0, 0, start=True)
            dve.wait_ge(u_init, C)
            row(1, 1)
            with dve.Fori(2, R - 3, 2) as r:
                row(r, 0)
                row(r + 1, 1)
            row(R - 2, 0)
            dve.wait_ge(cast_done[0], R)
            dve.wait_ge(cast_done[1], R)
            link(nc.vector.tensor_tensor(dis[:, :], deg[:, 0, :], deg[:, 1, :], ALU.add))
            nc.vector.tensor_scalar(dis[:, :], dis[:, :], 1.0 / BYTE_ONE, 1.0, ALU.mult, ALU.max).then_inc(deg_done, 1)
            row(R - 1, 1, last=True)
            dve.wait_ge(deg_root, 1)
            link(nc.vector.reciprocal(dis[:, :], dis[:, :]))
            link(nc.vector.tensor_scalar(norm[:, :], dis[:, :], x_up, None, ALU.mult))
            link(nc.vector.tensor_scalar(dis_out[:, :], dis[:, :], dif_scale, None, ALU.mult))
            dve.wait_ge(x_again, 32)
            dve.wait_ge(s_done, C * R)
            for q in range(C):
                xq = x2[:, q * TC:(q + 1) * TC, :]
                nc.vector.tensor_tensor(xq, xq, norm[:, q * TC:(q + 1) * TC].unsqueeze(2).to_broadcast([P, TC, D]),
                                        ALU.mult).then_inc(y_done, 1)
                if q == 0:
                    attn_add(R - 1)
                dve.wait_ge(y_hi, q + 1)
                nc.vector.tensor_tensor(y_parts[:, q * TC:(q + 1) * TC, D:2 * D], xq,
                                        y_parts[:, q * TC:(q + 1) * TC, 0:D], ALU.subtract).then_inc(y_lo, 1)

            def head(r, q, bank, base):
                dve.wait_ge(rows_done, r + (base + 1))
                hi, lo = ps_s[:, bank, 0:D], ps_s[:, bank, D:2 * D]
                if base == 0:
                    nc.vector.scalar_tensor_tensor(u[:, r, :], hi, dis_out[:, bass.ds(r, 1)], u[:, r, :],
                                                   ALU.mult, ALU.add).then_inc(hi_added, 1)
                    dve.wait_ge(hi_added, r + 1)
                    nc.vector.scalar_tensor_tensor(u[:, r, :], lo, dis_out[:, bass.ds(r, 1)], u[:, r, :],
                                                   ALU.mult, ALU.add).then_inc(sums_read, 1)
                    dve.wait_ge(sums_read, r + 1)
                else:
                    nc.vector.tensor_scalar(summed, hi, w_down, None, ALU.mult).then_inc(hi_added, 1)
                    dve.wait_ge(hi_added, r + (base + 1))
                    nc.vector.scalar_tensor_tensor(summed, lo, w_down, summed, ALU.mult, ALU.add).then_inc(sums_read, 1)
                    dve.wait_ge(sums_read, r + (base + 1))
                    nc.vector.scalar_tensor_tensor(u[:, r, :], summed, 0.0, u[:, r, :],
                                                   ALU.max, ALU.add).then_inc(relu_done, 1)
                    dve.wait_ge(relu_done, r + 1)
                nc.vector.bn_stats(stats[:, :], u[:, r, :]).wait_op(sign_done, 1, "sem-ge").then_inc(bn_done, 1)
                dve.wait_ge(bn_done, r + (base + 1))
                nc.vector.bn_aggr(mv[:, q, :], stats[:, :]).wait_op(sign_done, 1, "sem-ge").then_inc(var_done, 1)

            def normalise(r, q, base, wait=True):
                dve.wait_ge(std_done, r + (base + 1))
                nc.vector.reciprocal(rstd[:, q:q + 1], std[:, q:q + 1]).then_inc(rstd_done, 1)
                dve.wait_ge(rstd_done, r + (base + 1))
                if base == 0 and wait:
                    dve.wait_ge(x1_turned, r - 1)
                    dve.wait_ge(x1_kept, r - 1)
                nc.vector.tensor_scalar(x1_now[:, q, :] if base == 0 else u[:, r, :], u[:, r, :],
                                        mean[q], rstd[:, q:q + 1], ALU.subtract,
                                        ALU.mult).then_inc(x1_done if base == 0 else out_done, 1)

            def xw_low(r, q):
                dve.wait_ge(xw_hi, r + 1)
                nc.vector.scalar_tensor_tensor(x_parts[:, r, D:2 * D], xw_ps[q][:, 0:P], w_up,
                                               x_parts[:, r, 0:D], ALU.mult, ALU.subtract).then_inc(xw_lo, 1)

            def step(r, q, bank, lag):
                head(r, q, bank, 0)
                if lag >= 3:
                    xw_low(r - 3, 1 - q)
                if lag >= 1:
                    normalise(r - 1, 1 - q, 0, lag >= 3)
            for r in range(G):
                step(r, r % 2, r, r)
            with dve.Fori(G, R - G + 1, G) as r:
                for n in range(G):
                    step(r + n, n % 2, n, 3)
            normalise(R - 1, 1, 0)
            for r in range(R - 3, R):
                xw_low(r, r % 2)
            dve.wait_ge(x1_kept, R)
            head(0, 0, 0, R)
            for r in range(1, G):
                head(r, r % 2, r, R)
                normalise(r - 1, 1 - r % 2, R)
            with dve.Fori(G, R - G + 1, G) as r:
                for n in range(G):
                    head(r + n, n % 2, n, R)
                    normalise(r + (n - 1), 1 - n % 2, R)
            normalise(R - 1, 1, R)

        @block.tensor
        def _(pe):
            pe.wait_ge(ident_done, 1)
            for g in range(H):
                pe.wait_ge(xn_done, g // 2 + 1)
                if g >= 2:
                    pe.wait_ge(xnt_lo, g - 1)
                for n in range(TH):
                    t = TH * g + n
                    ins = nc.tensor.transpose(ps_e[:, g % 2, n * P:(n + 1) * P], scores[:, t * P:(t + 1) * P],
                                              ident[:, :])
                ins.then_inc(xnt_turned, 1)
                if g == 1:
                    pe.wait_ge(great_done, 1)
                    nc.tensor.transpose(ps_at[0:2, 0:P], great, ident[:, :]).then_inc(great_turned, 1)
                if g == 3:
                    pe.wait_ge(great_diag, 1)
                    nc.tensor.matmul(ps_at[:, 2 * P:2 * P + 2], ones2, pow2[0:2, :],
                                     start=True, stop=True).then_inc(great_spread, 1)

            def turn_adj(r, q, g, first=False):
                if first:
                    pe.wait_ge(scales_done, 1)
                pe.wait_ge(cast_done[g], r + 1)
                if not first:
                    pe.wait_ge(adj_stored, 2 * r + g)
                for n in range(TH):
                    b = TH * g + n
                    ins = nc.tensor.transpose(ps_at[:, n * P:(n + 1) * P], words[q][:, b * P:(b + 1) * P], ident[:, :])
                ins.then_inc(adj_turned, 1)

            def cosines(r, q, i, start=False):
                if start:
                    pe.wait_ge(xnt_lo, 2 * i + 2)
                if i == 0:
                    pe.wait_ge(signed, r + 1)
                if not (start and i < 2):
                    pe.wait_ge(scores_done, r * C + (i - 1))
                for part, other in ((0, 0), (0, 1), (1, 0)):
                    for n in range(2):
                        o = i * CH + n * BANK
                        ins = nc.tensor.matmul(ps_s[:, 2 * (i % 2) + n, :], xn_signed[:, q, part, :],
                                               xn_parts[:, other, o:o + BANK],
                                               start=(part == 0 and other == 0), stop=(part == 1))
                ins.then_inc(s_done, 1)

            def turn_e(r, h, start=False):
                if h % 2 == 0:
                    pe.wait_ge(exp_done, r * C + (h // 2 + 1))
                if not (start and h < 2):
                    pe.wait_ge(e_lo, r * H + (h - 1))
                for n in range(TH):
                    t = TH * h + n
                    ins = nc.tensor.transpose(ps_e[:, h % 2, n * P:(n + 1) * P], scores[:, t * P:(t + 1) * P],
                                              ident[:, :])
                ins.then_inc(e_turned, 1)

            def attend(r, h, start=False):
                pe.wait_ge(e_lo, r * H + (h + 1))
                if h == 0 and not start:
                    pe.wait_ge(attn_read, r)
                if start and h % 2 == 0:
                    pe.wait_ge(x_lo, h // 2 + 1)
                for n in range(TH):
                    t = TH * h + n
                    nc.tensor.matmul(ps_acc[:, 0:2 * D], eT_parts[:, h % 2, 0, n * P:(n + 1) * P], x_parts[:, t, :],
                                     start=(t == 0), stop=(t == R - 1), skip_group_check=True)
                    ins = nc.tensor.matmul(ps_acc[:, 0:D], eT_parts[:, h % 2, 1, n * P:(n + 1) * P],
                                           x_parts[:, t, 0:D], start=False, stop=(t == R - 1), skip_group_check=True)
                ins.then_inc(attn_part, 1)

            def row(r, q, start=False, last=False):
                if not last:
                    turn_adj(r + 1, 1 - q, 0)
                    cosines(r + 1, 1 - q, 0)
                    cosines(r + 1, 1 - q, 1)
                    turn_adj(r + 1, 1 - q, 1)
                turn_e(r, 0, start)
                turn_e(r, 1, start)
                for h in range(2, H):
                    turn_e(r, h)
                    attend(r, h - 2, start)
                    if h == 3 and not last:
                        cosines(r + 1, 1 - q, 2)
                    if h == 5 and not last:
                        cosines(r + 1, 1 - q, 3)
                attend(r, H - 2, start)
                attend(r, H - 1, start)

            turn_adj(0, 0, 0, first=True)
            for i in range(2):
                cosines(0, 0, i, start=True)
            turn_adj(0, 0, 1)
            for i in range(2, C):
                cosines(0, 0, i, start=True)
            row(0, 0, start=True)
            row(1, 1)
            with pe.Fori(2, R - 3, 2) as r:
                row(r, 0)
                row(r + 1, 1)
            row(R - 2, 0)
            row(R - 1, 1, last=True)

            def add_tile(bank, lhs, t, y):
                b, k = t // K, t % K
                return nc.tensor.matmul(ps_s[:, bank, 0:2 * D], lhs[:, b, :, k], y[:, t, :],
                                        start=(t == 0), stop=(t == R - 1))

            def whole_row(r, q, bank, y, base, layer, lead):
                pe.wait_ge(staged, r + (layer * (R - G) - G + 1))
                pe.wait_ge(sums_read, r + (base + 1 - G))
                for t in range(R):
                    ins = add_tile(bank, stage8[q], t, y)
                    if t == 0:
                        ins.wait_op(ident_done, 1, "sem-ge")
                ins.then_inc(rows_done, 1)

            def turn_x1(r, q):
                pe.wait_ge(x1_done, r + 1)
                nc.tensor.transpose(ps_e[:, q, 0:P], x1_now[:, q, :], ident[:, :]).then_inc(x1_turned, 1)

            def x1_w(r, q):
                pe.wait_ge(x1t_done, r + 1)
                nc.tensor.matmul(xw_ps[q][:, 0:P], x1t[:, q, :], wts,
                                 start=True, stop=True).then_inc(xw_done, 1)

            pe.wait_ge(scores_done, C * R)
            for t in range(R):
                if t % TC == 0:
                    pe.wait_ge(y_lo, t // TC + 1)
                for r in range(G):
                    ins = add_tile(r, adjT8[r], t, y_parts)
                    if t == R - 1:
                        ins.then_inc(rows_done, 1)
            pe.wait_ge(w_loaded, 32)

            def tail(r, q, lag):
                if lag >= 2:
                    if lag >= 4:
                        pe.wait_ge(x1t_done, r - 3)
                    turn_x1(r - 2, q)
                if lag >= 3:
                    x1_w(r - 3, 1 - q)

            for r in range(2, G):
                tail(r, r % 2, r)
            with pe.Fori(G, R - G + 1, G) as r:
                for n in range(G):
                    whole_row(r + n, n % 2, n, y_parts, 0, 0, n)
                    tail(r + n, n % 2, 4)
            turn_x1(R - 2, 0)
            x1_w(R - 3, 1)
            turn_x1(R - 1, 1)
            pe.wait_ge(xw_lo, R - 3)
            x1_w(R - 2, 0)
            pe.wait_ge(xw_lo, R - 2)
            x1_w(R - 1, 1)
            for t in range(R):
                if t >= R - TH:
                    pe.wait_ge(xw_lo, t + 1)
                if t == 0:
                    pe.wait_ge(xw_lo, R - TH)
                    pe.wait_ge(sums_read, R)
                for r in range(G):
                    ins = add_tile(r, adjT8[r], t, x_parts)
                    if t == R - 1:
                        ins.then_inc(rows_done, 1)
            with pe.Fori(G, R - G + 1, G) as r:
                for n in range(G):
                    whole_row(r + n, n % 2, n, x_parts, R, 1, n)


_INS = ["x", "adj", "L0_gnn_alpha", "L0_gnn_beta", "L1_gnn_weights"]


def kernel(**inputs):
    import numpy as _np
    import concourse.bacc as _bacc
    from concourse import mybir as _mybir
    from concourse.bass_utils import run_bass_kernel_spmd as _run

    nc = _bacc.Bacc("TRN2", target_bir_lowering=False, num_devices=1, dynamic_dma_scratch_size=1024)
    arrays, args = {}, []
    for name in _INS:
        a = _np.ascontiguousarray(inputs[name])
        arrays[f"in_{name}"] = a
        args.append(nc.dram_tensor(f"in_{name}", a.shape, _mybir.dt.from_np(a.dtype), kind="ExternalInput").ap())
    res = nc.dram_tensor("out_0", (4096, 128), _mybir.dt.float32, kind="ExternalOutput").ap()
    two_layer_gnn(nc, *args, res)
    r = _run(nc, [arrays], core_ids=[0])
    return r.results[0]["out_0"]
```

```python
from contextlib import ExitStack

import concourse.bass as bass
from concourse import mybir

ALU = mybir.AluOpType
ACT = mybir.ActivationFunctionType
AX = mybir.AxisListType
F32 = mybir.dt.float32
F16 = mybir.dt.float16
F8 = mybir.dt.float8e4
U8 = mybir.dt.uint8
U32 = mybir.dt.uint32
I32 = mybir.dt.int32

P = 128
K = 4
BANK = 512
BYTE_ONE = 64.0
BYTE_F8 = 2.0
XN_SCALE = 64.0
E_SCALE = 4096.0
X_SCALE = 4096.0
W_SCALE = 128.0
LN_EPS = 1e-5
MIN_NORM = 1e-8
LOWEST = -3.0e38


def two_layer_gnn(nc, x, adj, alpha, beta, weights, out):
    N, D = x.shape
    R = N // P
    B = R // K
    CH = 1024
    C = N // CH
    TC = CH // P
    H = N // BANK
    TH = BANK // P
    LAG = 3
    G = 4
    assert D == P and C == 4 and H == 8 and R == 32 and B == 8

    with ExitStack() as ctx:
        def sb(name, shape, dt):
            return ctx.enter_context(nc.sbuf_tensor(name, shape, dt))

        def psum(name, shape, dt):
            return ctx.enter_context(nc.psum_tensor(name, shape, dt))

        def sem(name):
            return ctx.enter_context(nc.semaphore(name))

        adjT = sb("adjT", [P, R, B, P], U32)
        land = sb("land", [P, 2, CH], F32)
        adj_bytes = sb("adj_bytes", [P, 2, N], U8)
        x_parts = sb("x_parts", [P, R, 2 * D], F16)
        xn_parts = sb("xn_parts", [P, 2, N], F16)
        xn_signed = sb("xn_signed", [P, 2, 2, P], F16)
        scores = sb("scores", [P, N], F32)
        u = sb("u", [P, R, D], F32)
        eT_parts = sb("eT_parts", [P, 4, 2, BANK], F16)
        ident = sb("ident", [P, P], F32)
        col = sb("col", [P, 26], F32)
        norm = sb("norm", [P, R], F32)
        deg = sb("deg", [P, C, R], F32)
        dis = sb("dis", [P, R], F32)
        dis_out = sb("dis_out", [P, R], F32)
        cmax = sb("cmax", [P, H], F32)
        csum = sb("csum", [P, C], F32)
        stats = sb("stats", [P, 6], F32)
        mv = sb("mv", [P, 2, 2], F32)

        def c(n):
            return col[:, n:n + 1]
        alpha_c, beta_c, e_alpha, sigma, neg_sigma, abs_beta = (c(n) for n in range(6))
        neg_max, total, r_total, gain = (c(n) for n in range(6, 10))
        attn_scale, x_up, dif_scale, w_up, w_down, eps_c = (c(n) for n in range(10, 16))
        great = col[:, 16:18]
        pow2 = col[:, 18:20]
        rpow2 = col[:, 20:22]
        std = col[:, 22:24]
        sign_beta, top = c(24), c(25)
        rstd = sb("rstd", [P, 2], F32)
        norm_r = sb("norm_r", [P, R], F32)

        ps_s = psum("ps_s", [P, 2, BANK], F32)
        ps_e = psum("ps_e", [P, 4, BANK], F32)
        ps_acc = psum("ps_acc", [P, BANK], F32)
        ps_at = psum("ps_at", [P, BANK], F32)

        x_loaded = [sem(f"x_loaded{q}") for q in range(C)]
        small_loaded = sem("small_loaded")
        w_loaded = sem("w_loaded")
        land_full = [sem("land_full0"), sem("land_full1")]
        x_again = [sem("x_again0"), sem("x_again1")]
        ident_zero = sem("ident_zero")
        ident_done = sem("ident_done")
        squares_done = sem("squares_done")
        norms2_done = sem("norms2_done")
        root_done = sem("root_done")
        dve_step = sem("dve_step")
        rnorm_done = sem("rnorm_done")
        xn_done = [sem(f"xn_done{q}") for q in range(C)]
        hi_scaled = sem("hi_scaled")
        xnt_turned = sem("xnt_turned")
        xnt_hi = sem("xnt_hi")
        xnt_lo = sem("xnt_lo")
        sign_done = sem("sign_done")
        signed = sem("signed")
        top_done = sem("top_done")
        great_done = sem("great_done")
        great_turned = sem("great_turned")
        great_diag = sem("great_diag")
        great_spread = sem("great_spread")
        scales_done = sem("scales_done")
        alpha_exp = sem("alpha_exp")
        sigma_done = sem("sigma_done")
        x_hi = sem("x_hi")
        x_lo = sem("x_lo")
        u_init = sem("u_init")
        cast_done = sem("cast_done")
        adj_turned = sem("adj_turned")
        adj_stored = sem("adj_stored")
        s_done = sem("s_done")
        scores_done = sem("scores_done")
        max_done = sem("max_done")
        exp_done = sem("exp_done")
        e_turned = sem("e_turned")
        e_hi = sem("e_hi")
        e_lo = sem("e_lo")
        attn_part = sem("attn_part")
        u_half = sem("u_half")
        attn_read = sem("attn_read")
        total_done = sem("total_done")
        deg_done = sem("deg_done")
        deg_root = sem("deg_root")
        dis_done = sem("dis_done")
        y_done = sem("y_done")
        y_hi = sem("y_hi")
        y_lo = sem("y_lo")
        staged = sem("staged")
        rows_done = sem("rows_done")
        sums_read = sem("sums_read")
        hi_added = sem("hi_added")
        bn_done = sem("bn_done")
        var_done = sem("var_done")
        std_done = sem("std_done")
        rstd_done = sem("rstd_done")
        x1_done = sem("x1_done")
        x1_turned = sem("x1_turned")
        x1_kept = sem("x1_kept")
        out_done = sem("out_done")
        x1t_done = sem("x1t_done")
        xw_done = sem("xw_done")
        xw_hi = sem("xw_hi")
        xw_lo = sem("xw_lo")
        relu_done = sem("relu_done")
        out_stored = sem("out_stored")

        x_v = x.rearrange("(b p k) d -> p b (k d)", p=P, k=K)
        out_v = out.rearrange("(b p k) d -> b p (k d)", p=P, k=K)
        adj_v = adj.rearrange("(b p k) j -> b k p j", p=P, k=K)
        u_b = u[:, :, :].rearrange("p (b k) d -> p b (k d)", k=K)
        x2 = land[:, :, :].rearrange("p h (r d) -> p h r d", d=D)
        y_parts = xn_parts[:, :, :].rearrange("p a (r d) -> p (a r) d", d=2 * D)
        x1t = scores[:, 0:2 * P].rearrange("p (a d) -> p a d", d=P)
        x1_now = scores[:, 2 * P:6 * P].rearrange("p (a d) -> p a d", d=P)
        wts = scores[:, 6 * P:7 * P]
        summed = scores[:, 7 * P:9 * P].rearrange("p (a d) -> p a d", d=P)
        xw_ps = [ps_acc, ps_at]
        wts_early = eT_parts[:, 0, 0, 0:2 * P].bitcast(F32)
        ones2 = eT_parts[0:2, 1, 1, 0:2 * P].bitcast(F32)
        mean = [mv[:, q, 0:1] for q in range(2)]
        var = [mv[:, q, 1:2] for q in range(2)]
        words = [adj_bytes[:, q, :].bitcast(F32) for q in range(2)]
        stage = [adj_bytes[:, q, :].bitcast(U32) for q in range(2)]
        stage8 = [adj_bytes[:, q, :].bitcast(F8).rearrange("p (b i k) -> p b i k", b=B, k=K) for q in range(2)]
        adjT8 = [adjT[:, r, :, :].rearrange("p b i -> p (b i)").bitcast(F8)
                 .rearrange("p (b i k) -> p b i k", b=B, k=K) for r in range(G)]
        adjT_rows = adjT[:, :, :, :].rearrange("p r b i -> p r (b i)")

        block = ctx.enter_context(nc.Block())

        @block.sync
        def _(sp):
            sp.dma_start(u_b[:, 0:2, :], x_v[:, 0:2, :]).then_inc(x_loaded[0], 16)
            sp.dma_start(alpha_c, alpha.rearrange("(a o) -> a o", o=1).to_broadcast([P, 1])).then_inc(small_loaded, 16)
            sp.dma_start(beta_c, beta.rearrange("(a o) -> a o", o=1).to_broadcast([P, 1])).then_inc(small_loaded, 16)
            for q in range(1, C):
                sp.dma_start(u_b[:, 2 * q:2 * q + 2, :], x_v[:, 2 * q:2 * q + 2, :]).then_inc(x_loaded[q], 16)
            sp.dma_start(wts_early, weights).then_inc(w_loaded, 16)

            def land_piece(b, k, i):
                sp.dma_start(land[:, i % 2, :], adj_v[b, k, :, i * CH:(i + 1) * CH]).then_inc(land_full[i % 2], 16)
            for k in range(K):
                for i in range(C):
                    if k * C + i >= 2:
                        sp.wait_ge(cast_done, k * C + (i - 1))
                    land_piece(0, k, i)
            with sp.Fori(1, B) as b:
                for k in range(K):
                    for i in range(C):
                        sp.wait_ge(cast_done, b * (K * C) + (k * C + i - 1))
                        land_piece(b, k, i)
            for q in range(C):
                if q < 2:
                    sp.wait_ge(cast_done, C * R - 1 + q)
                else:
                    sp.wait_ge(y_lo, q - 1)
                sp.dma_start(land[:, q % 2, :].rearrange("p (b x) -> p b x", b=2),
                             x_v[:, 2 * q:2 * q + 2, :]).then_inc(x_again[q % 2], 16)
            sp.wait_ge(e_turned, R * H)
            sp.dma_start(wts, weights).then_inc(w_loaded, 16)
            with sp.Fori(0, B) as b:
                sp.wait_ge(out_done, b * K + K)
                sp.dma_start(out_v[b], u_b[:, b, :]).then_inc(out_stored, 16)
            sp.wait_ge(out_stored, 16 * B)

        @block.gpsimd
        def _(pool):
            nc.gpsimd.memset(ones2, 1.0)
            nc.gpsimd.memset(ident[:, :], 0.0).then_inc(ident_zero, 1)
            pool.wait_ge(ident_zero, 1)
            nc.gpsimd.affine_select(out=ident[:, :], in_=ident[:, :], compare_op=ALU.not_equal, fill=1.0, base=0,
                                    pattern=[[-1, P]], channel_multiplier=1).then_inc(ident_done, 1)

            def unit_rows(q):
                pool.wait_ge(rnorm_done, q + 1)
                nc.gpsimd.tensor_tensor(
                    scores[:, q * CH:(q + 1) * CH].rearrange("p (r d) -> p r d", d=D), u[:, q * TC:(q + 1) * TC, :],
                    norm_r[:, q * TC:(q + 1) * TC].unsqueeze(2).to_broadcast([P, TC, D]),
                    ALU.mult).then_inc(xn_done[q], 1)

            def sign_block(r, q, first=False):
                if not first:
                    pool.wait_ge(s_done, r * H - H)
                nc.gpsimd.tensor_tensor(xn_signed[:, q, :, :], xn_parts[:, :, bass.ds(r * P, P)],
                                        sign_beta.unsqueeze(2).to_broadcast([P, 2, P]), ALU.mult).then_inc(signed, 1)

            unit_rows(1)
            unit_rows(3)
            pool.wait_ge(sign_done, 1)
            pool.wait_ge(xnt_lo, 1)
            sign_block(0, 0, first=True)
            sign_block(1, 1, first=True)
            pool.wait_ge(sigma_done, 1)
            for q in range(C):
                pool.wait_ge(xn_done[q], 1)
                pool.wait_ge(x_lo, q + 1)
                v = u[:, q * TC:(q + 1) * TC, :].rearrange("p r d -> p (r d)")
                nc.gpsimd.tensor_scalar(v, v, neg_sigma, 1.0, ALU.mult, ALU.mult).then_inc(u_init, 1)
            with pool.Fori(2, R - 1, 2) as r:
                sign_block(r, 0)
                sign_block(r + 1, 1)

        @block.scalar
        def _(act):
            for q in range(C):
                act.wait_ge(x_loaded[q], 16)
                nc.scalar.activation(scores[:, q * CH:(q + 1) * CH],
                                     u[:, q * TC:(q + 1) * TC, :].rearrange("p r d -> p (r d)"),
                                     ACT.Square).then_inc(squares_done, 1)
            for q in range(C):
                act.wait_ge(norms2_done, q + 1)
                nc.scalar.activation(norm[:, q * TC:(q + 1) * TC], norm[:, q * TC:(q + 1) * TC], ACT.Sqrt,
                                     scale=1.0 / (XN_SCALE * XN_SCALE)).then_inc(root_done, 1)

            def cast(r, q, i):
                act.wait_ge(land_full[i % 2], r * 32 + 16 * (i // 2 + 1))
                nc.scalar.activation(adj_bytes[:, q, i * CH:(i + 1) * CH], land[:, i % 2, :], ACT.Copy,
                                     scale=BYTE_ONE, accum_out=deg[:, i, bass.ds(r, 1)]).then_inc(cast_done, 1)

            for g in range(H):
                act.wait_ge(xnt_turned, g + 1)
                nc.scalar.activation(xn_parts[:, 0, g * BANK:(g + 1) * BANK], ps_e[:, g % 4, :],
                                     ACT.Copy).then_inc(xnt_hi, 1)
                if g % 2 == 1:
                    cast(0, 0, g // 2)
            act.wait_ge(small_loaded, 32)
            nc.scalar.activation(e_alpha, alpha_c, ACT.Exp, scale=-1.0).then_inc(alpha_exp, 1)
            act.wait_ge(scales_done, 1)
            for q in range(C):
                nc.scalar.activation(x_parts[:, q * TC:(q + 1) * TC, 0:D], u[:, q * TC:(q + 1) * TC, :],
                                     ACT.Copy, scale=x_up).then_inc(x_hi, 1)
                cast(1, 1, q)

            def exps(r, i):
                if i == 0:
                    act.wait_ge(max_done, r + 1)
                nc.scalar.activation(scores[:, i * CH:(i + 1) * CH], scores[:, i * CH:(i + 1) * CH], ACT.Exp,
                                     bias=neg_max, scale=abs_beta, accum_out=csum[:, i:i + 1]).then_inc(exp_done, 1)

            def e_high(r, h, start):
                act.wait_ge(e_turned, r * H + (h + 1))
                if not (start and h < 4):
                    act.wait_ge(attn_part, r * H + (h - 3))
                nc.scalar.activation(eT_parts[:, h % 4, 0, :], ps_e[:, h % 4, :], ACT.Copy,
                                     scale=E_SCALE).then_inc(e_hi, 1)

            def y_high(q):
                act.wait_ge(y_done, q + 1)
                nc.scalar.activation(y_parts[:, q * TC:(q + 1) * TC, 0:D], x2[:, q % 2, :, :],
                                     ACT.Copy).then_inc(y_hi, 1)

            CASTS = (3, 4, 6, 7)
            def row(r, q, start=False):
                exps(r, 0)
                exps(r, 1)
                for h in range(H):
                    e_high(r, h, start)
                    if h == 1:
                        exps(r, 2)
                    if h == 2:
                        exps(r, 3)
                    if h in CASTS:
                        cast(r + 2, q, CASTS.index(h))

            def late_row(r, q):
                exps(r, 0)
                exps(r, 1)
                for h in range(H):
                    e_high(r, h, False)
                    if h == 1:
                        exps(r, 2)
                    if h == 3:
                        exps(r, 3)
                        if r == R - 1:
                            act.wait_ge(deg_done, 1)
                            nc.scalar.activation(dis[:, :], dis[:, :], ACT.Sqrt).then_inc(deg_root, 1)
                    if r == R - 1 and h in (4, 5):
                        y_high(h - 4)

            row(0, 0, start=True)
            row(1, 1)
            with act.Fori(2, R - 3, 2) as r:
                row(r, 0)
                row(r + 1, 1)
            late_row(R - 2, 0)
            late_row(R - 1, 1)
            y_high(2)
            y_high(3)

            def root(r, q, base):
                act.wait_ge(var_done, r + (base + 1))
                nc.scalar.activation(std[:, q:q + 1], var[q], ACT.Sqrt, bias=eps_c).then_inc(std_done, 1)

            def turned_out(r, n):
                act.wait_ge(x1_done, r + 1)
                nc.scalar.activation(u[:, r, :], x1_now[:, n, :], ACT.Copy).then_inc(x1_kept, 1)
                act.wait_ge(x1_turned, r + 1)
                nc.scalar.activation(x1t[:, n % 2, :], ps_s[:, n % 2, 0:P], ACT.Copy).then_inc(x1t_done, 1)

            def xw_high(r, n):
                act.wait_ge(xw_done, r + 1)
                nc.scalar.activation(x_parts[:, r, 0:D], xw_ps[n % 2][:, 0:P], ACT.Copy,
                                     scale=w_up).then_inc(xw_hi, 1)

            def step(r, n, lag):
                if lag >= 5:
                    xw_high(r - 5, (n + 3) % G)
                if lag >= 4:
                    turned_out(r - 4, n)
                root(r, n % 2, 0)
            for r in range(2 * G):
                step(r, r % G, r)
            with act.Fori(2 * G, R - G + 1, G) as r:
                for n in range(G):
                    step(r + n, n, 5)
            for r in range(R - G, R):
                xw_high(r - 1, (r - 1) % G)
                turned_out(r, r % G)
            xw_high(R - 1, (R - 1) % G)

            def sum_high(r, n):
                act.wait_ge(rows_done, r + (R + 1))
                nc.scalar.activation(summed[:, n % 2, :], ps_e[:, n, 0:D], ACT.Copy, scale=w_down).then_inc(hi_scaled, 1)
            sum_high(0, 0)
            for r in range(1, G):
                sum_high(r, r)
                root(r - 1, (r - 1) % 2, R)
            with act.Fori(G, R - G + 1, G) as r:
                for n in range(G):
                    sum_high(r + n, n)
                    root(r + (n - 1), (n + 1) % 2, R)
            root(R - 1, 1, R)

        @block.vector
        def _(dve):
            steps = [0]

            def link(ins):
                steps[0] += 1
                ins.then_inc(dve_step, 1)
                dve.wait_ge(dve_step, steps[0])

            nc.vector.memset(eps_c, LN_EPS).then_inc(xw_lo, 2)
            dve.wait_ge(small_loaded, 32)
            link(nc.vector.tensor_scalar(sign_beta, beta_c, 0.0, 2.0, ALU.is_ge, ALU.mult))
            link(nc.vector.tensor_scalar(sign_beta, sign_beta, -1.0, None, ALU.add))
            nc.vector.tensor_scalar(abs_beta, beta_c, sign_beta, None, ALU.mult).then_inc(sign_done, 1)
            def norms2(q):
                dve.wait_ge(squares_done, q + 1)
                link(nc.vector.tensor_reduce(norm[:, q * TC:(q + 1) * TC],
                                             scores[:, q * CH:(q + 1) * CH].rearrange("p (r d) -> p r d", d=D),
                                             AX.X, ALU.add))
                nc.vector.tensor_scalar(norm[:, q * TC:(q + 1) * TC], norm[:, q * TC:(q + 1) * TC],
                                        MIN_NORM * MIN_NORM, None, ALU.max).then_inc(norms2_done, 1)

            def rnorm(q):
                dve.wait_ge(root_done, q + 1)
                nc.vector.reciprocal(norm_r[:, q * TC:(q + 1) * TC], norm[:, q * TC:(q + 1) * TC]).then_inc(rnorm_done, 1)

            def unit_rows(q):
                dve.wait_ge(rnorm_done, q + 1)
                nc.vector.tensor_tensor(
                    scores[:, q * CH:(q + 1) * CH].rearrange("p (r d) -> p r d", d=D), u[:, q * TC:(q + 1) * TC, :],
                    norm_r[:, q * TC:(q + 1) * TC].unsqueeze(2).to_broadcast([P, TC, D]),
                    ALU.mult).then_inc(xn_done[q], 1)

            def xnt_low(g):
                dve.wait_ge(xnt_hi, g + 1)
                nc.vector.tensor_tensor(xn_parts[:, 1, g * BANK:(g + 1) * BANK], ps_e[:, g % 4, :],
                                        xn_parts[:, 0, g * BANK:(g + 1) * BANK], ALU.subtract).then_inc(xnt_lo, 1)

            norms2(0)
            norms2(1)
            rnorm(0)
            unit_rows(0)
            rnorm(1)
            norms2(2)
            norms2(3)
            rnorm(2)
            rnorm(3)
            unit_rows(2)
            xnt_low(0)
            xnt_low(1)
            dve.wait_ge(w_loaded, 16)
            link(nc.vector.tensor_reduce(great[:, 1:2], wts_early, AX.X, ALU.max, apply_absolute_value=True))
            nc.vector.tensor_reduce(great[:, 0:1], norm[:, :], AX.X, ALU.max).then_inc(great_done, 1)
            xnt_low(2)
            xnt_low(3)
            dve.wait_ge(great_turned, 1)
            link(nc.vector.tensor_reduce(top[0:2, :], ps_at[0:2, 0:P], AX.X, ALU.max))
            nc.vector.tensor_scalar(pow2[0:2, :], ident[0:2, 0:2], top[0:2, :], None,
                                    ALU.mult).then_inc(great_diag, 1)
            xnt_low(4)
            xnt_low(5)
            dve.wait_ge(great_spread, 1)
            link(nc.vector.tensor_scalar(pow2, ps_at[:, 2 * P:2 * P + 2], 1e-30, 1e30, ALU.max, ALU.min))
            link(nc.vector.tensor_scalar(pow2.bitcast(I32), pow2.bitcast(I32), 0x7F800000, None, ALU.bitwise_and))
            link(nc.vector.reciprocal(rpow2, pow2))
            nc.vector.tensor_scalar(x_up, rpow2[:, 0:1], X_SCALE / XN_SCALE, None, ALU.mult).then_inc(scales_done, 1)
            dve.wait_ge(scales_done, 1)
            xnt_low(6)
            xnt_low(7)

            def store_adj(r, g):
                dve.wait_ge(adj_turned, 2 * r + (g + 1))
                nc.vector.tensor_copy(adjT_rows[:, r, g * BANK:(g + 1) * BANK],
                                      ps_at[:, :].bitcast(U32)).then_inc(adj_stored, 1)

            def mask(r, q, h, start=False):
                dve.wait_ge(s_done, r * H + (h + 1))
                if not start:
                    dve.wait_ge(e_turned, r * H + (h + 1 - H))
                dve.wait_ge(cast_done, r * C + (h // 2 + 1))
                o = h * BANK
                nc.vector.tensor_tensor_reduce(
                    scores[:, o:o + BANK].rearrange("p (k q) -> p k q", k=K),
                    ps_s[:, h % 2, :].rearrange("p (k q) -> p k q", k=K),
                    adj_bytes[:, q, o:o + BANK].rearrange("p (q k) -> p k q", k=K),
                    1.0 / (XN_SCALE * XN_SCALE * BYTE_ONE), LOWEST, ALU.mult, ALU.max, cmax[:, h:h + 1]
                ).wait_op(sign_done, 1, "sem-ge").then_inc(scores_done, 1)

            def row_max(r):
                dve.wait_ge(scores_done, r * H + H)
                nc.vector.tensor_reduce(top, cmax[:, :], AX.X, ALU.max, negate=True).then_inc(top_done, 1)
                dve.wait_ge(top_done, r + 1)
                nc.vector.tensor_scalar(neg_max, top, abs_beta, None, ALU.mult).then_inc(max_done, 1)

            def e_low(r, h):
                dve.wait_ge(e_hi, r * H + (h + 1))
                nc.vector.scalar_tensor_tensor(eT_parts[:, h % 4, 1, :], ps_e[:, h % 4, :], E_SCALE,
                                               eT_parts[:, h % 4, 0, :], ALU.mult, ALU.subtract).then_inc(e_lo, 1)

            def attn_add(r):
                dve.wait_ge(attn_part, r * H + H)
                dve.wait_ge(total_done, 3 * r + 3)
                nc.vector.scalar_tensor_tensor(u[:, r, :], ps_acc[:, 0:D], gain, u[:, r, :],
                                               ALU.mult, ALU.add).then_inc(u_half, 1)
                dve.wait_ge(u_half, r + 1)
                nc.vector.scalar_tensor_tensor(u[:, r, :], ps_acc[:, D:2 * D], gain, u[:, r, :],
                                               ALU.mult, ALU.add).then_inc(attn_read, 1)

            def total_step(r, n):
                if n == 0:
                    dve.wait_ge(exp_done, r * C + C)
                    ins = nc.vector.tensor_reduce(total, csum[:, :], AX.X, ALU.add)
                elif n == 1:
                    dve.wait_ge(total_done, 3 * r + 1)
                    ins = nc.vector.reciprocal(r_total, total)
                else:
                    dve.wait_ge(total_done, 3 * r + 2)
                    ins = nc.vector.tensor_scalar(gain, r_total, attn_scale, None, ALU.mult)
                ins.then_inc(total_done, 1)

            def x_low(q):
                dve.wait_ge(x_hi, q + 1)
                nc.vector.scalar_tensor_tensor(x_parts[:, q * TC:(q + 1) * TC, D:2 * D],
                                               u[:, q * TC:(q + 1) * TC, :], x_up,
                                               x_parts[:, q * TC:(q + 1) * TC, 0:D],
                                               ALU.mult, ALU.subtract).then_inc(x_lo, 1)

            store_adj(0, 0)
            for h in range(H):
                mask(0, 0, h, start=True)
                if h == 1:
                    store_adj(0, 1)
            row_max(0)
            dve.wait_ge(alpha_exp, 1)
            link(nc.vector.tensor_scalar(sigma, e_alpha, 1.0, None, ALU.add))
            link(nc.vector.reciprocal(sigma, sigma))
            nc.vector.tensor_scalar(neg_sigma, sigma, -1.0, None, ALU.mult).then_inc(sigma_done, 1)
            link(nc.vector.tensor_scalar(w_up, rpow2[:, 1:2], W_SCALE, None, ALU.mult))
            link(nc.vector.tensor_scalar(w_down, pow2[:, 1:2], 1.0 / (W_SCALE * BYTE_F8), None, ALU.mult))
            link(nc.vector.tensor_scalar(dif_scale, pow2[:, 0:1], XN_SCALE / (X_SCALE * BYTE_F8), None, ALU.mult))
            link(nc.vector.tensor_scalar(attn_scale, pow2[:, 0:1], sigma, XN_SCALE / (X_SCALE * E_SCALE),
                                         ALU.mult, ALU.mult))

            def row(r, q, start=False):
                for h in range(H):
                    if start and h % 2 == 0:
                        x_low(h // 2)
                    if h == 2 and not start:
                        attn_add(r - 1)
                    mask(r + 1, 1 - q, h)
                    if h == H - 1:
                        row_max(r + 1)
                    if h in (0, 2):
                        store_adj(r + 1, h // 2)
                    e_low(r, h)
                    if 4 <= h <= 6:
                        total_step(r, h - 4)

            def stage_block(r, q):
                nc.vector.tensor_copy(stage[q], adjT_rows[:, r, :]).then_inc(staged, 1)

            def y_high_scale(q):
                dve.wait_ge(x_again[q % 2], 16 * (q // 2 + 1))
                nc.vector.tensor_tensor(x2[:, q % 2, :, :], x2[:, q % 2, :, :],
                                        norm_r[:, q * TC:(q + 1) * TC].unsqueeze(2).to_broadcast([P, TC, D]),
                                        ALU.mult).then_inc(y_done, 1)

            def y_low(q):
                dve.wait_ge(y_hi, q + 1)
                nc.vector.tensor_tensor(y_parts[:, q * TC:(q + 1) * TC, D:2 * D], x2[:, q % 2, :, :],
                                        y_parts[:, q * TC:(q + 1) * TC, 0:D], ALU.subtract).then_inc(y_lo, 1)

            row(0, 0, start=True)
            dve.wait_ge(u_init, C)
            row(1, 1)
            with dve.Fori(2, R - 3, 2) as r:
                row(r, 0)
                row(r + 1, 1)
            row(R - 2, 0)
            dve.wait_ge(cast_done, C * R)
            link(nc.vector.tensor_reduce(dis[:, :], deg[:, :, :].rearrange("p a r -> p r a"), AX.X, ALU.add))
            nc.vector.tensor_scalar(dis[:, :], dis[:, :], 1.0 / BYTE_ONE, 1.0, ALU.mult, ALU.max).then_inc(deg_done, 1)
            attn_add(R - 2)
            stage_block(G, 0)
            stage_block(G + 1, 1)
            for h in range(H):
                e_low(R - 1, h)
                if h == 3:
                    dve.wait_ge(deg_root, 1)
                    link(nc.vector.reciprocal(dis[:, :], dis[:, :]))
                    link(nc.vector.tensor_scalar(norm_r[:, :], dis[:, :], x_up, None, ALU.mult))
                    link(nc.vector.tensor_scalar(dis_out[:, :], dis[:, :], dif_scale, None, ALU.mult))
                    y_high_scale(0)
                if h == 4:
                    y_low(0)
                    y_high_scale(1)
                if h == 5:
                    y_low(1)
                if h >= 5:
                    total_step(R - 1, h - 5)
            y_high_scale(2)
            y_low(2)
            attn_add(R - 1)
            y_high_scale(3)
            y_low(3)

            def spread(r, q, base):
                dve.wait_ge(relu_done if base else sums_read, r + 1)
                nc.vector.bn_stats(stats[:, :], u[:, r, :]).wait_op(sign_done, 1, "sem-ge").then_inc(bn_done, 1)
                dve.wait_ge(bn_done, r + (base + 1))
                nc.vector.bn_aggr(mv[:, q, :], stats[:, :]).wait_op(sign_done, 1, "sem-ge").then_inc(var_done, 1)

            def head0(r, n):
                nc.vector.scalar_tensor_tensor(u[:, r, :], ps_e[:, n, 0:D], dis_out[:, bass.ds(r, 1)], u[:, r, :],
                                               ALU.mult, ALU.add).then_inc(hi_added, 1)
                dve.wait_ge(hi_added, r + 1)
                nc.vector.scalar_tensor_tensor(u[:, r, :], ps_e[:, n, D:2 * D], dis_out[:, bass.ds(r, 1)], u[:, r, :],
                                               ALU.mult, ALU.add).then_inc(sums_read, 1)
                spread(r, n % 2, 0)

            def head1(r, n):
                dve.wait_ge(hi_scaled, r + 1)
                nc.vector.scalar_tensor_tensor(summed[:, n % 2, :], ps_e[:, n, D:2 * D], w_down, summed[:, n % 2, :],
                                               ALU.mult, ALU.add).then_inc(sums_read, 1)
                dve.wait_ge(sums_read, r + (R + 1))
                nc.vector.scalar_tensor_tensor(u[:, r, :], summed[:, n % 2, :], 0.0, u[:, r, :],
                                               ALU.max, ALU.add).then_inc(relu_done, 1)
                spread(r, n % 2, R)

            def normalise(r, n, base, wait=True):
                q = n % 2
                dve.wait_ge(std_done, r + (base + 1))
                nc.vector.reciprocal(rstd[:, q:q + 1], std[:, q:q + 1]).then_inc(rstd_done, 1)
                dve.wait_ge(rstd_done, r + (base + 1))
                if base == 0 and wait:
                    dve.wait_ge(x1_turned, r - 3)
                    dve.wait_ge(x1_kept, r - 3)
                nc.vector.tensor_scalar(x1_now[:, n, :] if base == 0 else u[:, r, :], u[:, r, :],
                                        mean[q], rstd[:, q:q + 1], ALU.subtract,
                                        ALU.mult).then_inc(x1_done if base == 0 else out_done, 1)

            def xw_low(r, n):
                dve.wait_ge(xw_hi, r + 1)
                nc.vector.scalar_tensor_tensor(x_parts[:, r, D:2 * D], xw_ps[n % 2][:, 0:P], w_up,
                                               x_parts[:, r, 0:D], ALU.mult, ALU.subtract).then_inc(xw_lo, 1)

            def step(r, n, lag, more=True):
                dve.wait_ge(rows_done, r + 1)
                if lag >= G and more:
                    stage_block(r + 2, n % 2)
                head0(r, n)
                if lag >= 5:
                    xw_low(r - 5, (n + 3) % G)
                if lag >= 1:
                    normalise(r - 1, (n + 3) % G, 0, lag >= 5)
            for r in range(2 * G):
                step(r, r % G, r)
            with dve.Fori(2 * G, R - 2 * G + 1, G) as r:
                for n in range(G):
                    step(r + n, n, 5)
            for r in range(R - G, R):
                step(r, r % G, 5, r + 2 < R)
                if r + 2 >= R:
                    stage_block(G + r + 2 - R, r % 2)
            normalise(R - 1, (R - 1) % G, 0)
            for r in range(R - 5, R):
                xw_low(r, r % G)

            dve.wait_ge(x1_kept, R)

            def last_step(r, n, more=True, stage_next=True):
                dve.wait_ge(rows_done, r + (R + 1))
                if stage_next:
                    stage_block(r + 2, n % 2)
                head1(r, n)
                if more:
                    normalise(r - 1, (n + 3) % G, R)
            for r in range(G):
                last_step(r, r, r >= 1, False)
            with dve.Fori(G, R - 2 * G + 1, G) as r:
                for n in range(G):
                    last_step(r + n, n)
            for r in range(R - G, R):
                last_step(r, r % G, True, r + 2 < R)
            normalise(R - 1, (R - 1) % G, R)

        @block.tensor
        def _(pe):
            pe.wait_ge(ident_done, 1)
            for g in range(H):
                pe.wait_ge(xn_done[g // 2], 1)
                if g >= 4:
                    pe.wait_ge(xnt_lo, g - 3)
                for n in range(TH):
                    t = TH * g + n
                    ins = nc.tensor.transpose(ps_e[:, g % 4, n * P:(n + 1) * P], scores[:, t * P:(t + 1) * P],
                                              ident[:, :])
                ins.then_inc(xnt_turned, 1)
                if g == 5:
                    pe.wait_ge(great_done, 1)
                    nc.tensor.transpose(ps_at[0:2, 0:P], great, ident[:, :]).then_inc(great_turned, 1)
                if g == 6:
                    pe.wait_ge(great_diag, 1)
                    nc.tensor.matmul(ps_at[:, 2 * P:2 * P + 2], ones2, pow2[0:2, :],
                                     start=True, stop=True).then_inc(great_spread, 1)

            def turn_adj(r, q, g, first=False):
                if first:
                    pe.wait_ge(scales_done, 1)
                pe.wait_ge(cast_done, r * C + (2 * g + 2))
                if not first:
                    pe.wait_ge(adj_stored, 2 * r + g)
                for n in range(TH):
                    b = TH * g + n
                    ins = nc.tensor.transpose(ps_at[:, n * P:(n + 1) * P], words[q][:, b * P:(b + 1) * P], ident[:, :])
                ins.then_inc(adj_turned, 1)

            def cosines(r, q, h, start=False):
                if start:
                    pe.wait_ge(xnt_lo, h + 1)
                if h == 0:
                    pe.wait_ge(signed, r + 1)
                if not (start and h < 2):
                    pe.wait_ge(scores_done, r * H + (h - 1))
                o = h * BANK
                for part, other in ((0, 0), (0, 1), (1, 0)):
                    ins = nc.tensor.matmul(ps_s[:, h % 2, :], xn_signed[:, q, part, :], xn_parts[:, other, o:o + BANK],
                                           start=(part == 0 and other == 0), stop=(part == 1))
                ins.then_inc(s_done, 1)

            def turn_e(r, h, start=False):
                if h % 2 == 0:
                    pe.wait_ge(exp_done, r * C + (h // 2 + 1))
                if not (start and h < 4):
                    pe.wait_ge(e_lo, r * H + (h - 3))
                for n in range(TH):
                    t = TH * h + n
                    ins = nc.tensor.transpose(ps_e[:, h % 4, n * P:(n + 1) * P], scores[:, t * P:(t + 1) * P],
                                              ident[:, :])
                ins.then_inc(e_turned, 1)

            def attend(r, h, start=False):
                pe.wait_ge(e_lo, r * H + (h + 1))
                if h == 0 and not start:
                    pe.wait_ge(attn_read, r)
                if start and h % 2 == 0:
                    pe.wait_ge(x_lo, h // 2 + 1)
                for n in range(TH):
                    t = TH * h + n
                    nc.tensor.matmul(ps_acc[:, 0:2 * D], eT_parts[:, h % 4, 0, n * P:(n + 1) * P], x_parts[:, t, :],
                                     start=(t == 0), stop=(t == R - 1), skip_group_check=True)
                    ins = nc.tensor.matmul(ps_acc[:, 0:D], eT_parts[:, h % 4, 1, n * P:(n + 1) * P],
                                           x_parts[:, t, 0:D], start=False, stop=(t == R - 1), skip_group_check=True)
                ins.then_inc(attn_part, 1)

            def row(r, q, start=False, left=2):
                for h in range(H):
                    turn_e(r, h, start)
                    if left and h in (0, 2):
                        turn_adj(r + 1, 1 - q, h // 2)
                    if h >= LAG:
                        attend(r, h - LAG, start)
                    elif h == 1 and not start:
                        attend(r - 1, H - 1)
                    if left and 1 <= h < H - 1:
                        cosines(r + 1, 1 - q, h + 1)
                for h in range(H - LAG, H - 1):
                    attend(r, h, start)
                    if left > 1:
                        cosines(r + 2, q, h - (H - LAG))

            turn_adj(0, 0, 0, first=True)
            for h in range(H):
                cosines(0, 0, h, start=True)
                if h == 1:
                    turn_adj(0, 0, 1)
            cosines(1, 1, 0)
            cosines(1, 1, 1)
            row(0, 0, start=True)
            row(1, 1)
            with pe.Fori(2, R - 3, 2) as r:
                row(r, 0)
                row(r + 1, 1)
            row(R - 2, 0, left=1)
            row(R - 1, 1, left=0)
            attend(R - 1, H - 1)

            def add_tile(n, lhs, t, y):
                b, k = t // K, t % K
                return nc.tensor.matmul(ps_e[:, n, 0:2 * D], lhs[:, b, :, k], y[:, t, :],
                                        start=(t == 0), stop=(t == R - 1))

            def turn_x1(r, n):
                pe.wait_ge(x1_done, r + 1)
                nc.tensor.transpose(ps_s[:, n % 2, 0:P], x1_now[:, n, :], ident[:, :]).then_inc(x1_turned, 1)

            def x1_w(r, n):
                pe.wait_ge(x1t_done, r + 1)
                pe.wait_ge(xw_lo, r + 1)
                nc.tensor.matmul(xw_ps[n % 2][:, 0:P], x1t[:, n % 2, :], wts, start=True, stop=True).then_inc(xw_done, 1)

            def whole_row(r, n, y, layer):
                pe.wait_ge(staged, r + (layer * (R - G) - G + 1))
                pe.wait_ge(sums_read, r + (layer * R + 1 - G))
                for t in range(R):
                    ins = add_tile(n, stage8[n % 2], t, y)
                    if t == 0:
                        ins.wait_op(ident_done, 1, "sem-ge")
                    if layer == 0 and t == R // 2:
                        turn_x1(r - G, n)
                ins.then_inc(rows_done, 1)
                if layer == 0:
                    x1_w(r - G, n)

            pe.wait_ge(e_lo, R * H)
            for t in range(R):
                if t % TC == 0:
                    pe.wait_ge(y_lo, t // TC + 1)
                for r in range(G):
                    ins = add_tile(r, adjT8[r], t, y_parts)
                    if t == R - 1:
                        ins.then_inc(rows_done, 1)
            pe.wait_ge(w_loaded, 32)
            with pe.Fori(G, R - G + 1, G) as r:
                for n in range(G):
                    whole_row(r + n, n, y_parts, 0)
            for t in range(R):
                if t == 0:
                    pe.wait_ge(xw_lo, R - G - 1 + 2)
                if t >= R - G - 1:
                    pe.wait_ge(xw_lo, t + 1 + 2)
                for r in range(G):
                    if t == 0:
                        pe.wait_ge(sums_read, R - G + r + 1)
                    ins = add_tile(r, adjT8[r], t, x_parts)
                    if t == R - 1:
                        ins.then_inc(rows_done, 1)
                for n in range(G):
                    if t == 2 * n + 3:
                        turn_x1(R - G + n, n)
                    if t == 2 * n + 4:
                        x1_w(R - G + n, n)
            with pe.Fori(G, R - G + 1, G) as r:
                for n in range(G):
                    whole_row(r + n, n, x_parts, 1)


_INS = ["x", "adj", "L0_gnn_alpha", "L0_gnn_beta", "L1_gnn_weights"]


def kernel(**inputs):
    import numpy as _np
    import concourse.bacc as _bacc
    from concourse import mybir as _mybir
    from concourse.bass_utils import run_bass_kernel_spmd as _run

    nc = _bacc.Bacc("TRN2", target_bir_lowering=False, num_devices=1, dynamic_dma_scratch_size=1024)
    arrays, args = {}, []
    for name in _INS:
        a = _np.ascontiguousarray(inputs[name])
        arrays[f"in_{name}"] = a
        args.append(nc.dram_tensor(f"in_{name}", a.shape, _mybir.dt.from_np(a.dtype), kind="ExternalInput").ap())
    res = nc.dram_tensor("out_0", (4096, 128), _mybir.dt.float32, kind="ExternalOutput").ap()
    two_layer_gnn(nc, *args, res)
    r = _run(nc, [arrays], core_ids=[0])
    return r.results[0]["out_0"]
```

```python
from contextlib import ExitStack

import concourse.bass as bass
from concourse import mybir

ALU = mybir.AluOpType
ACT = mybir.ActivationFunctionType
AX = mybir.AxisListType
F32 = mybir.dt.float32
F16 = mybir.dt.float16
F8 = mybir.dt.float8e4
U8 = mybir.dt.uint8
U32 = mybir.dt.uint32
I32 = mybir.dt.int32

P = 128
K = 4
BANK = 512
BYTE_ONE = 64
BYTE_F8 = 2.0
XN_SCALE = 64.0
E_SCALE = 4096.0
X_SCALE = 4096.0
W_SCALE = 128.0
LN_EPS = 1e-5
MIN_NORM = 1e-8
LOWEST = -3.0e38


def two_layer_gnn(nc, x, adj, alpha, beta, weights, out):
    N, D = x.shape
    R = N // P
    B = R // K
    CH = 1024
    C = N // CH
    TC = CH // P
    H = N // BANK
    TH = BANK // P
    LAG = 3
    G = 4
    assert D == P and C == 4 and H == 8 and R == 32 and B == 8

    with ExitStack() as ctx:
        def sb(name, shape, dt):
            return ctx.enter_context(nc.sbuf_tensor(name, shape, dt))

        def psum(name, shape, dt):
            return ctx.enter_context(nc.psum_tensor(name, shape, dt))

        def sem(name):
            return ctx.enter_context(nc.semaphore(name))

        adjT = sb("adjT", [P, R, B, P], U32)
        land = sb("land", [P, 2, CH], F32)
        adj_bytes = sb("adj_bytes", [P, 2, N], U8)
        x_parts = sb("x_parts", [P, R, 2 * D], F16)
        xn_parts = sb("xn_parts", [P, 2, N], F16)
        xn_signed = sb("xn_signed", [P, 2, 2, P], F16)
        scores = sb("scores", [P, N], F32)
        u = sb("u", [P, R, D], F32)
        eT_parts = sb("eT_parts", [P, 4, 2, BANK], F16)
        ident = sb("ident", [P, P], F32)
        col = sb("col", [P, 29], F32)
        packed = sb("packed", [P, CH // K], U32)
        norm = sb("norm", [P, R], F32)
        norm_r = sb("norm_r", [P, R], F32)
        deg = sb("deg", [P, C, R], F32)
        dis = sb("dis", [P, R], F32)
        dis_out = sb("dis_out", [P, R], F32)
        cmax = sb("cmax", [P, H], F32)
        csum = sb("csum", [P, C], F32)
        stats = sb("stats", [P, 6], F32)
        mv = sb("mv", [P, 2, 2], F32)

        def c(n):
            return col[:, n:n + 1]
        alpha_c, beta_c, e_alpha, sigma, u_scale, abs_beta = (c(n) for n in range(6))
        neg_max, total, r_total, gain = (c(n) for n in range(6, 10))
        attn_scale, x_up, dif_scale, w_up, w_down, eps_c = (c(n) for n in range(10, 16))
        great = col[:, 16:18]
        pow2 = col[:, 18:20]
        rpow2 = col[:, 20:22]
        std = col[:, 22:24]
        sign_beta, top = c(24), c(25)
        table_loads = [c(26), c(27), c(28)]
        rstd = sb("rstd", [P, 2], F32)

        ps_s = psum("ps_s", [P, 2, BANK], F32)
        ps_e = psum("ps_e", [P, 4, BANK], F32)
        ps_acc = psum("ps_acc", [P, BANK], F32)
        ps_at = psum("ps_at", [P, BANK], F32)

        x_loaded = [sem(f"x_loaded{q}") for q in range(C)]
        small_loaded = sem("small_loaded")
        eps_set = sem("eps_set")
        w_loaded = sem("w_loaded")
        land_full = [sem("land_full0"), sem("land_full1")]
        x_again = [sem(f"x_again{q}") for q in range(C)]
        ident_zero = sem("ident_zero")
        ident_done = sem("ident_done")
        squares_done = sem("squares_done")
        norms2_done = sem("norms2_done")
        root_done = sem("root_done")
        dve_step = sem("dve_step")
        rnorm_done = sem("rnorm_done")
        xn_done = [sem(f"xn_done{q}") for q in range(C)]
        hi_scaled = sem("hi_scaled")
        xnt_turned = sem("xnt_turned")
        xnt_hi = sem("xnt_hi")
        xnt_lo = sem("xnt_lo")
        sign_done = sem("sign_done")
        signed = sem("signed")
        top_done = sem("top_done")
        great_done = sem("great_done")
        great_turned = sem("great_turned")
        great_diag = sem("great_diag")
        great_spread = sem("great_spread")
        scales_done = sem("scales_done")
        alpha_exp = sem("alpha_exp")
        sigma_done = sem("sigma_done")
        x_scaled = sem("x_scaled")
        x_hi = sem("x_hi")
        x_lo = sem("x_lo")
        u_init = sem("u_init")
        cast_done = sem("cast_done")
        pack_step = sem("pack_step")
        packed_done = sem("packed_done")
        adj_turned = sem("adj_turned")
        adj_stored = sem("adj_stored")
        s_done = sem("s_done")
        scores_done = sem("scores_done")
        max_done = sem("max_done")
        exp_done = sem("exp_done")
        e_turned = sem("e_turned")
        e_hi = sem("e_hi")
        e_lo = sem("e_lo")
        attn_part = sem("attn_part")
        u_half = sem("u_half")
        attn_read = sem("attn_read")
        total_done = sem("total_done")
        deg_done = sem("deg_done")
        deg_root = sem("deg_root")
        dis_done = sem("dis_done")
        y_done = sem("y_done")
        y_hi = sem("y_hi")
        y_lo = sem("y_lo")
        staged = sem("staged")
        rows_done = sem("rows_done")
        sums_read = sem("sums_read")
        hi_added = sem("hi_added")
        bn_done = sem("bn_done")
        var_done = sem("var_done")
        std_done = sem("std_done")
        rstd_done = sem("rstd_done")
        x1_done = sem("x1_done")
        x1_turned = sem("x1_turned")
        x1_kept = sem("x1_kept")
        out_done = sem("out_done")
        x1t_done = sem("x1t_done")
        xw_done = sem("xw_done")
        xw_hi = sem("xw_hi")
        xw_lo = sem("xw_lo")
        relu_done = sem("relu_done")
        out_stored = sem("out_stored")

        x_v = x.rearrange("(b p k) d -> p b (k d)", p=P, k=K)
        out_v = out.rearrange("(b p k) d -> b p (k d)", p=P, k=K)
        adj_v = adj.rearrange("(b p k) j -> b k p j", p=P, k=K)
        u_b = u[:, :, :].rearrange("p (b k) d -> p b (k d)", k=K)
        x_again_at = ([land[:, q, :].rearrange("p (r d) -> p r d", d=D) for q in range(2)]
                      + [adj_bytes[:, q, :].bitcast(F32).rearrange("p (r d) -> p r d", d=D) for q in range(2)])
        y_parts = xn_parts[:, :, :].rearrange("p a (r d) -> p r a d", d=D)
        x1t = scores[:, 0:2 * P].rearrange("p (a d) -> p a d", d=P)
        x1_now = scores[:, 2 * P:6 * P].rearrange("p (a d) -> p a d", d=P)
        wts = scores[:, 6 * P:7 * P]
        summed = scores[:, 7 * P:9 * P].rearrange("p (a d) -> p a d", d=P)
        xw_ps = [ps_acc, ps_at]
        wts_early = eT_parts[:, 0, 0, 0:2 * P].bitcast(F32)
        ones2 = eT_parts[0:2, 1, 1, 0:2 * P].bitcast(F32)
        mean = [mv[:, q, 0:1] for q in range(2)]
        var = [mv[:, q, 1:2] for q in range(2)]
        words = [adj_bytes[:, q, :].bitcast(U32).rearrange("p (i w) -> p i w", i=C) for q in range(2)]
        packed_f = packed[:, :].bitcast(F32)
        stage = [adj_bytes[:, q, :].bitcast(U32) for q in range(2)]
        stage8 = [adj_bytes[:, q, :].bitcast(F8).rearrange("p (b i k) -> p b i k", b=B, k=K) for q in range(2)]
        adjT8 = [adjT[:, r, :, :].rearrange("p b i -> p (b i)").bitcast(F8)
                 .rearrange("p (b i k) -> p b i k", b=B, k=K) for r in range(G)]
        adjT_rows = adjT[:, :, :, :].rearrange("p r b i -> p r (b i)")

        def score_bank(h, start):
            return ps_e[:, h - 2 if h < 4 else h - 4, :] if start and h % 4 >= 2 else ps_s[:, h % 2, :]

        block = ctx.enter_context(nc.Block())

        @block.sync
        def _(sp):
            sp.dma_start(u_b[:, 0:2, :], x_v[:, 0:2, :]).then_inc(x_loaded[0], 16)
            sp.dma_start(alpha_c, alpha.rearrange("(a o) -> a o", o=1).to_broadcast([P, 1])).then_inc(small_loaded, 16)
            sp.dma_start(beta_c, beta.rearrange("(a o) -> a o", o=1).to_broadcast([P, 1])).then_inc(small_loaded, 16)
            for q in range(1, C):
                sp.dma_start(u_b[:, 2 * q:2 * q + 2, :], x_v[:, 2 * q:2 * q + 2, :]).then_inc(x_loaded[q], 16)
            sp.dma_start(wts_early, weights).then_inc(w_loaded, 16)

            def land_piece(b, k, i):
                sp.dma_start(land[:, i % 2, :], adj_v[b, k, :, i * CH:(i + 1) * CH]).then_inc(land_full[i % 2], 16)
            for k in range(K):
                for i in range(C):
                    if k * C + i >= 2:
                        sp.wait_ge(cast_done, k * C + (i - 1))
                    land_piece(0, k, i)
            with sp.Fori(1, B) as b:
                for k in range(K):
                    for i in range(C):
                        sp.wait_ge(cast_done, b * (K * C) + (k * C + i - 1))
                        land_piece(b, k, i)
            for q in range(C):
                if q < 2:
                    sp.wait_ge(cast_done, C * R - 1 + q)
                else:
                    sp.wait_ge(scores_done, (R - 3 + q) * H)
                    sp.wait_ge(packed_done, R - 3 + q)
                sp.dma_start(x_again_at[q].rearrange("p (b k) d -> p b (k d)", b=2),
                             x_v[:, 2 * q:2 * q + 2, :]).then_inc(x_again[q], 16)
            sp.wait_ge(e_turned, R * H)
            sp.dma_start(wts, weights).then_inc(w_loaded, 16)
            with sp.Fori(0, B - 1) as b:
                sp.wait_ge(out_done, b * K + K)
                sp.dma_start(out_v[b], u_b[:, b, :]).then_inc(out_stored, 16)
            for part, r in ((slice(0, 3 * D), R - 1), (slice(3 * D, 4 * D), R)):
                sp.wait_ge(out_done, r)
                sp.dma_start(out_v[B - 1, :, part], u_b[:, B - 1, part]).then_inc(out_stored, 16)
            sp.wait_ge(out_stored, 16 * (B + 1))

        @block.gpsimd
        def _(pool):
            nc.gpsimd.memset(ones2, 1.0)
            nc.gpsimd.memset(ident[:, :], 0.0).then_inc(ident_zero, 1)
            pool.wait_ge(ident_zero, 1)
            nc.gpsimd.affine_select(out=ident[:, :], in_=ident[:, :], compare_op=ALU.not_equal, fill=1.0, base=0,
                                    pattern=[[-1, P]], channel_multiplier=1).then_inc(ident_done, 1)

            def unit_rows(q):
                pool.wait_ge(rnorm_done, q + 1)
                nc.gpsimd.tensor_tensor(
                    scores[:, q * CH:(q + 1) * CH].rearrange("p (r d) -> p r d", d=D), u[:, q * TC:(q + 1) * TC, :],
                    norm_r[:, q * TC:(q + 1) * TC].unsqueeze(2).to_broadcast([P, TC, D]),
                    ALU.mult).then_inc(xn_done[q], 1)

            def sign_block(r, q, first=False):
                if not first:
                    pool.wait_ge(s_done, r * H - H)
                nc.gpsimd.tensor_tensor(xn_signed[:, q, :, :], xn_parts[:, :, bass.ds(r * P, P)],
                                        sign_beta.unsqueeze(2).to_broadcast([P, 2, P]), ALU.mult).then_inc(signed, 1)

            def pack(r, q, first=False):
                pool.wait_ge(cast_done, r * C + C)
                if not first:
                    pool.wait_ge(adj_turned, r)
                nc.gpsimd.tensor_tensor(packed[:, :], words[q][:, 0, :], words[q][:, 1, :],
                                        ALU.add).then_inc(pack_step, 1)
                pool.wait_ge(pack_step, 2 * r + 1)
                nc.gpsimd.tensor_tensor(packed[:, :], packed[:, :], words[q][:, 2, :],
                                        ALU.add).then_inc(pack_step, 1)
                pool.wait_ge(pack_step, 2 * r + 2)
                nc.gpsimd.tensor_tensor(packed[:, :], packed[:, :], words[q][:, 3, :],
                                        ALU.add).then_inc(packed_done, 1)

            unit_rows(1)
            unit_rows(3)
            pool.wait_ge(sign_done, 1)
            pool.wait_ge(xnt_lo, 1)
            sign_block(0, 0, first=True)
            sign_block(1, 1, first=True)
            pool.wait_ge(scales_done, 1)
            for q in range(C):
                x_q, x_both = u[:, q * TC:(q + 1) * TC, :], x_parts[:, q * TC:(q + 1) * TC, :]
                pool.wait_ge(xn_done[q], 1)
                nc.gpsimd.tensor_scalar(x_q, x_q, x_up, 1.0, ALU.mult, ALU.mult).then_inc(x_scaled, 1)
                pool.wait_ge(x_scaled, q + 1)
                nc.gpsimd.tensor_scalar(x_both[:, :, 0:D], x_q, 1.0, 1.0, ALU.mult, ALU.mult).then_inc(x_hi, 1)
                pool.wait_ge(x_hi, q + 1)
                nc.gpsimd.tensor_tensor(x_both[:, :, D:2 * D], x_q, x_both[:, :, 0:D], ALU.subtract).then_inc(x_lo, 1)
                if q == 0:
                    pack(0, 0, first=True)
            sign_block(2, 0)
            pack(1, 1)
            pool.wait_ge(sigma_done, 1)
            for q in range(C):
                pool.wait_ge(x_lo, q + 1)
                v = u[:, q * TC:(q + 1) * TC, :].rearrange("p r d -> p (r d)")
                nc.gpsimd.tensor_scalar(v, v, u_scale, 1.0, ALU.mult, ALU.mult).then_inc(u_init, 1)
            with pool.Fori(2, R - 3, 2) as r:
                pack(r, 0)
                sign_block(r + 1, 1)
                pack(r + 1, 1)
                sign_block(r + 2, 0)
            pack(R - 2, 0)
            sign_block(R - 1, 1)
            pack(R - 1, 1)
            pool.wait_ge(dis_done, 1)
            for q in range(C):
                pool.wait_ge(x_again[q], 16)
                y_q = x_again_at[q]
                nc.gpsimd.tensor_tensor(y_q, y_q, norm_r[:, q * TC:(q + 1) * TC].unsqueeze(2).to_broadcast([P, TC, D]),
                                        ALU.mult).then_inc(y_done, 1)
                pool.wait_ge(y_done, q + 1)
                pool.wait_ge(s_done, (R - 1) * H + 2 * q + 2)
                nc.gpsimd.tensor_scalar(y_parts[:, q * TC:(q + 1) * TC, 0, :], y_q, 1.0, 1.0,
                                        ALU.mult, ALU.mult).then_inc(y_hi, 1)

        @block.scalar
        def _(act):
            def squares(q):
                act.wait_ge(x_loaded[q], 16)
                nc.scalar.activation(scores[:, q * CH:(q + 1) * CH],
                                     u[:, q * TC:(q + 1) * TC, :].rearrange("p r d -> p (r d)"),
                                     ACT.Square).then_inc(squares_done, 1)

            def block_squares(q):
                act.wait_ge(x_loaded[q], 16)
                for r in range(q * TC, (q + 1) * TC):
                    ins = nc.scalar.activation(scores[:, r * P:(r + 1) * P], u[:, r, :], ACT.Square,
                                               accum_out=norm[:, r:r + 1])
                ins.then_inc(squares_done, 1)

            def norm_root(q):
                act.wait_ge(norms2_done, q + 1)
                nc.scalar.activation(norm[:, q * TC:(q + 1) * TC], norm[:, q * TC:(q + 1) * TC], ACT.Sqrt,
                                     scale=1.0 / (XN_SCALE * XN_SCALE)).then_inc(root_done, 1)

            def cast(r, q, i, first=False):
                if not first:
                    act.wait_ge(packed_done, r - 1)
                act.wait_ge(land_full[i % 2], r * 32 + 16 * (i // 2 + 1))
                nc.scalar.activation(adj_bytes[:, q, i * CH:(i + 1) * CH], land[:, i % 2, :], ACT.Copy,
                                     scale=float(BYTE_ONE >> i), accum_out=deg[:, i, bass.ds(r, 1)]).then_inc(cast_done, 1)

            act.wait_ge(eps_set, 1)
            nc.scalar.activation(table_loads[0], eps_c, ACT.Sqrt)
            squares(0)
            squares(1)
            norm_root(0)
            squares(2)
            norm_root(1)
            block_squares(3)
            norm_root(2)
            cast(0, 0, 0, first=True)
            norm_root(3)

            for g in range(H):
                act.wait_ge(xnt_turned, g + 1)
                nc.scalar.activation(xn_parts[:, 0, g * BANK:(g + 1) * BANK], ps_e[:, g % 4, :],
                                     ACT.Copy).then_inc(xnt_hi, 1)
                if g % 2 == 1:
                    cast((g // 2 + 1) // C, (g // 2 + 1) // C, (g // 2 + 1) % C, first=True)
            act.wait_ge(small_loaded, 32)
            nc.scalar.activation(e_alpha, alpha_c, ACT.Exp, scale=-1.0).then_inc(alpha_exp, 1)
            act.wait_ge(scales_done, 1)
            cast(1, 1, 1, first=True)
            cast(1, 1, 2, first=True)

            def exps(r, i):
                if i == 0:
                    act.wait_ge(max_done, r + 1)
                nc.scalar.activation(scores[:, i * CH:(i + 1) * CH], scores[:, i * CH:(i + 1) * CH], ACT.Exp,
                                     bias=neg_max, scale=abs_beta, accum_out=csum[:, i:i + 1]).then_inc(exp_done, 1)

            def e_high(r, h, start):
                act.wait_ge(e_turned, r * H + (h + 1))
                if not (start and h < 4):
                    act.wait_ge(attn_part, r * H + (h - 3))
                nc.scalar.activation(eT_parts[:, h % 4, 0, :], ps_e[:, h % 4, :], ACT.Copy,
                                     scale=E_SCALE).then_inc(e_hi, 1)

            def row(r, q, start=False):
                casts = (4, 5, 6, 7) if start else (3, 4, 6, 7)
                exps(r, 0)
                exps(r, 1)
                for h in range(H):
                    if start and h == 2:
                        cast(1, 1, 3, first=True)
                    e_high(r, h, start)
                    if h == 1:
                        exps(r, 2)
                    if h == 2:
                        exps(r, 3)
                    if h in casts:
                        cast(r + 2, q, casts.index(h))

            def late_row(r, q):
                exps(r, 0)
                exps(r, 1)
                for h in range(H):
                    e_high(r, h, False)
                    if h == 1:
                        exps(r, 2)
                    if h == 2:
                        exps(r, 3)
                    if r == R - 2 and h == 3:
                        act.wait_ge(deg_done, 1)
                        nc.scalar.activation(dis[:, :], dis[:, :], ACT.Sqrt).then_inc(deg_root, 1)
                    if h == H - 2:
                        nc.scalar.activation(table_loads[1 + q], eps_c, ACT.Sqrt if q else ACT.Exp)

            row(0, 0, start=True)
            row(1, 1)
            with act.Fori(2, R - 3, 2) as r:
                row(r, 0)
                row(r + 1, 1)
            late_row(R - 2, 0)
            late_row(R - 1, 1)

            def root(r, q, base):
                act.wait_ge(var_done, r + (base + 1))
                nc.scalar.activation(std[:, q:q + 1], var[q], ACT.Sqrt, bias=eps_c).then_inc(std_done, 1)

            def turned_out(r, n):
                act.wait_ge(x1_done, r + 1)
                nc.scalar.activation(u[:, r, :], x1_now[:, n, :], ACT.Copy).then_inc(x1_kept, 1)
                act.wait_ge(x1_turned, r + 1)
                nc.scalar.activation(x1t[:, n % 2, :], ps_s[:, n % 2, 0:P], ACT.Copy).then_inc(x1t_done, 1)

            def xw_high(r, n):
                act.wait_ge(xw_done, r + 1)
                nc.scalar.activation(x_parts[:, r, 0:D], xw_ps[n % 2][:, 0:P], ACT.Copy,
                                     scale=w_up).then_inc(xw_hi, 1)

            def step(r, n, lag):
                if lag >= 5:
                    xw_high(r - 5, (n + 3) % G)
                if lag >= 4:
                    turned_out(r - 4, n)
                root(r, n % 2, 0)
            for r in range(2 * G):
                step(r, r % G, r)
            with act.Fori(2 * G, R - G + 1, G) as r:
                for n in range(G):
                    step(r + n, n, 5)
            for r in range(R - G, R):
                xw_high(r - 1, (r - 1) % G)
                turned_out(r, r % G)
            xw_high(R - 1, (R - 1) % G)

            def sum_high(r, n):
                act.wait_ge(rows_done, r + (R + 1))
                nc.scalar.activation(summed[:, n % 2, :], ps_e[:, n, 0:D], ACT.Copy, scale=w_down).then_inc(hi_scaled, 1)
            sum_high(0, 0)
            for r in range(1, G):
                sum_high(r, r)
                root(r - 1, (r - 1) % 2, R)
            with act.Fori(G, R - G + 1, G) as r:
                for n in range(G):
                    sum_high(r + n, n)
                    root(r + (n - 1), (n + 1) % 2, R)
            root(R - 1, 1, R)

        @block.vector
        def _(dve):
            steps = [0]

            def link(ins):
                steps[0] += 1
                ins.then_inc(dve_step, 1)
                dve.wait_ge(dve_step, steps[0])

            nc.vector.memset(eps_c, LN_EPS).then_inc(eps_set, 1)
            nc.vector.memset(top, 0.0).then_inc(xw_lo, 2)
            dve.wait_ge(small_loaded, 32)
            link(nc.vector.tensor_scalar(sign_beta, beta_c, 0.0, 2.0, ALU.is_ge, ALU.mult))
            link(nc.vector.tensor_scalar(sign_beta, sign_beta, -1.0, None, ALU.add))
            nc.vector.tensor_scalar(abs_beta, beta_c, sign_beta, None, ALU.mult).then_inc(sign_done, 1)

            def norms2(q):
                dve.wait_ge(squares_done, q + 1)
                if q < C - 1:
                    link(nc.vector.tensor_reduce(norm[:, q * TC:(q + 1) * TC],
                                                 scores[:, q * CH:(q + 1) * CH].rearrange("p (r d) -> p r d", d=D),
                                                 AX.X, ALU.add))
                nc.vector.tensor_scalar(norm[:, q * TC:(q + 1) * TC], norm[:, q * TC:(q + 1) * TC],
                                        MIN_NORM * MIN_NORM, None, ALU.max).then_inc(norms2_done, 1)

            def rnorm(q):
                dve.wait_ge(root_done, q + 1)
                nc.vector.reciprocal(norm_r[:, q * TC:(q + 1) * TC], norm[:, q * TC:(q + 1) * TC]).then_inc(rnorm_done, 1)

            def unit_rows(q):
                dve.wait_ge(rnorm_done, q + 1)
                nc.vector.tensor_tensor(
                    scores[:, q * CH:(q + 1) * CH].rearrange("p (r d) -> p r d", d=D), u[:, q * TC:(q + 1) * TC, :],
                    norm_r[:, q * TC:(q + 1) * TC].unsqueeze(2).to_broadcast([P, TC, D]),
                    ALU.mult).then_inc(xn_done[q], 1)

            def xnt_low(g):
                dve.wait_ge(xnt_hi, g + 1)
                nc.vector.tensor_tensor(xn_parts[:, 1, g * BANK:(g + 1) * BANK], ps_e[:, g % 4, :],
                                        xn_parts[:, 0, g * BANK:(g + 1) * BANK], ALU.subtract).then_inc(xnt_lo, 1)

            norms2(0)
            norms2(1)
            rnorm(0)
            rnorm(1)
            unit_rows(0)
            norms2(2)
            rnorm(2)
            unit_rows(2)
            norms2(3)
            rnorm(3)
            xnt_low(0)
            xnt_low(1)
            dve.wait_ge(w_loaded, 16)
            link(nc.vector.tensor_reduce(great[:, 1:2], wts_early, AX.X, ALU.max, apply_absolute_value=True))
            nc.vector.tensor_reduce(great[:, 0:1], norm[:, :], AX.X, ALU.max).then_inc(great_done, 1)
            xnt_low(2)
            xnt_low(3)
            dve.wait_ge(great_turned, 1)
            link(nc.vector.tensor_reduce(top[0:2, :], ps_at[0:2, 0:P], AX.X, ALU.max))
            nc.vector.tensor_scalar(pow2[0:2, :], ident[0:2, 0:2], top[0:2, :], None,
                                    ALU.mult).then_inc(great_diag, 1)
            xnt_low(4)
            xnt_low(5)
            dve.wait_ge(great_spread, 1)
            link(nc.vector.tensor_scalar(pow2, ps_at[:, 2 * P:2 * P + 2], 1e-30, 1e30, ALU.max, ALU.min))
            link(nc.vector.tensor_scalar(pow2.bitcast(I32), pow2.bitcast(I32), 0x7F800000, None, ALU.bitwise_and))
            link(nc.vector.reciprocal(rpow2, pow2))
            nc.vector.tensor_scalar(x_up, rpow2[:, 0:1], X_SCALE / XN_SCALE, None, ALU.mult).then_inc(scales_done, 1)
            dve.wait_ge(scales_done, 1)
            xnt_low(6)
            xnt_low(7)

            def store_adj(r, i):
                if i == 0:
                    dve.wait_ge(adj_turned, r + 1)
                nc.vector.tensor_scalar(adjT_rows[:, r, i * CH // K:(i + 1) * CH // K],
                                        ps_at[:, 0:CH // K].bitcast(U32), i, BYTE_ONE * 0x01010101,
                                        ALU.logical_shift_left, ALU.bitwise_and).then_inc(adj_stored, 1)

            def mask(r, q, h, start=False):
                dve.wait_ge(s_done, r * H + (h + 1))
                if not start:
                    dve.wait_ge(e_turned, r * H + (h + 1 - H))
                dve.wait_ge(cast_done, r * C + (h // 2 + 1))
                o = h * BANK
                nc.vector.tensor_tensor_reduce(
                    scores[:, o:o + BANK].rearrange("p (k q) -> p k q", k=K),
                    score_bank(h, start).rearrange("p (k q) -> p k q", k=K),
                    adj_bytes[:, q, o:o + BANK].rearrange("p (q k) -> p k q", k=K),
                    1.0 / (XN_SCALE * XN_SCALE * (BYTE_ONE >> (h // 2))), LOWEST, ALU.mult, ALU.max, cmax[:, h:h + 1]
                ).wait_op(sign_done, 1, "sem-ge").then_inc(scores_done, 1)

            def row_max(r):
                dve.wait_ge(scores_done, r * H + H)
                nc.vector.tensor_reduce(top, cmax[:, :], AX.X, ALU.max, negate=True).then_inc(top_done, 1)
                dve.wait_ge(top_done, r + 1)
                nc.vector.tensor_scalar(neg_max, top, abs_beta, None, ALU.mult).then_inc(max_done, 1)

            def e_low(r, h):
                dve.wait_ge(e_hi, r * H + (h + 1))
                nc.vector.scalar_tensor_tensor(eT_parts[:, h % 4, 1, :], ps_e[:, h % 4, :], E_SCALE,
                                               eT_parts[:, h % 4, 0, :], ALU.mult, ALU.subtract).then_inc(e_lo, 1)

            def attn_add(r):
                dve.wait_ge(attn_part, r * H + H)
                dve.wait_ge(total_done, 3 * r + 3)
                nc.vector.scalar_tensor_tensor(u[:, r, :], ps_acc[:, 0:D], gain, u[:, r, :],
                                               ALU.mult, ALU.add).then_inc(u_half, 1)
                dve.wait_ge(u_half, r + 1)
                nc.vector.scalar_tensor_tensor(u[:, r, :], ps_acc[:, D:2 * D], gain, u[:, r, :],
                                               ALU.mult, ALU.add).then_inc(attn_read, 1)

            def total_step(r, n):
                if n == 0:
                    dve.wait_ge(exp_done, r * C + C)
                    ins = nc.vector.tensor_reduce(total, csum[:, :], AX.X, ALU.add)
                elif n == 1:
                    dve.wait_ge(total_done, 3 * r + 1)
                    ins = nc.vector.reciprocal(r_total, total)
                else:
                    dve.wait_ge(total_done, 3 * r + 2)
                    ins = nc.vector.tensor_scalar(gain, r_total, attn_scale, None, ALU.mult)
                ins.then_inc(total_done, 1)

            for h in range(H):
                mask(0, 0, h, start=True)
            row_max(0)
            dve.wait_ge(alpha_exp, 1)
            link(nc.vector.tensor_scalar(sigma, e_alpha, 1.0, None, ALU.add))
            link(nc.vector.reciprocal(sigma, sigma))
            nc.vector.tensor_scalar(u_scale, pow2[:, 0:1], sigma, -XN_SCALE / X_SCALE,
                                    ALU.mult, ALU.mult).then_inc(sigma_done, 1)
            link(nc.vector.tensor_scalar(w_up, rpow2[:, 1:2], W_SCALE, None, ALU.mult))
            link(nc.vector.tensor_scalar(w_down, pow2[:, 1:2], 1.0 / (W_SCALE * BYTE_F8), None, ALU.mult))
            link(nc.vector.tensor_scalar(dif_scale, pow2[:, 0:1], XN_SCALE / (X_SCALE * BYTE_F8), None, ALU.mult))
            link(nc.vector.tensor_scalar(attn_scale, pow2[:, 0:1], sigma, XN_SCALE / (X_SCALE * E_SCALE),
                                         ALU.mult, ALU.mult))

            def row(r, q, start=False, second=False, degrees=False):
                for h in range(H):
                    if degrees and h < C - 1:
                        if h == 0:
                            dve.wait_ge(cast_done, C * R)
                        link(nc.vector.scalar_tensor_tensor(dis[:, :], deg[:, h + 1, :], float(2 << h),
                                                            dis[:, :] if h else deg[:, 0, :], ALU.mult, ALU.add))
                    if degrees and h == 2:
                        nc.vector.tensor_scalar(dis[:, :], dis[:, :], 1.0 / BYTE_ONE, 1.0,
                                                ALU.mult, ALU.max).then_inc(deg_done, 1)
                    if degrees and h == 4:
                        dve.wait_ge(deg_root, 1)
                        link(nc.vector.reciprocal(dis[:, :], dis[:, :]))
                        nc.vector.tensor_scalar(norm_r[:, :], dis[:, :], x_up, None, ALU.mult).then_inc(dis_done, 1)
                        nc.vector.tensor_scalar(dis_out[:, :], dis[:, :], dif_scale, None, ALU.mult).then_inc(dis_done, 1)
                    if h == 2 and not start:
                        if second:
                            dve.wait_ge(u_init, C)
                        attn_add(r - 1)
                    mask(r + 1, 1 - q, h)
                    if h == H - 1:
                        row_max(r + 1)
                    e_low(r, h)
                    if h >= 4:
                        store_adj(r, h - 4)
                    if h >= 5:
                        total_step(r, h - 5)

            def stage_block(r, q):
                nc.vector.tensor_copy(stage[q], adjT_rows[:, r, :]).then_inc(staged, 1)

            def y_low(q):
                dve.wait_ge(y_hi, q + 1)
                nc.vector.tensor_tensor(y_parts[:, q * TC:(q + 1) * TC, 1, :], x_again_at[q],
                                        y_parts[:, q * TC:(q + 1) * TC, 0, :], ALU.subtract).then_inc(y_lo, 1)

            row(0, 0, start=True)
            row(1, 1, second=True)
            with dve.Fori(2, R - 3, 2) as r:
                row(r, 0)
                row(r + 1, 1)
            row(R - 2, 0, degrees=True)
            y_low(0)
            for h in range(H):
                if h == 2:
                    attn_add(R - 2)
                if h == 3:
                    y_low(1)
                if h == 5:
                    y_low(2)
                e_low(R - 1, h)
                if 4 <= h <= 6:
                    total_step(R - 1, h - 4)
            y_low(3)
            attn_add(R - 1)
            for i in range(C):
                store_adj(R - 1, i)
            dve.wait_ge(y_lo, C)
            stage_block(G, 0)
            stage_block(G + 1, 1)
            dve.wait_ge(dis_done, 2)

            def spread(r, q, base):
                dve.wait_ge(relu_done if base else sums_read, r + 1)
                nc.vector.bn_stats(stats[:, :], u[:, r, :]).wait_op(sign_done, 1, "sem-ge").then_inc(bn_done, 1)
                dve.wait_ge(bn_done, r + (base + 1))
                nc.vector.bn_aggr(mv[:, q, :], stats[:, :]).wait_op(sign_done, 1, "sem-ge").then_inc(var_done, 1)

            def head0(r, n):
                nc.vector.scalar_tensor_tensor(u[:, r, :], ps_e[:, n, 0:D], dis_out[:, bass.ds(r, 1)], u[:, r, :],
                                               ALU.mult, ALU.add).then_inc(hi_added, 1)
                dve.wait_ge(hi_added, r + 1)
                nc.vector.scalar_tensor_tensor(u[:, r, :], ps_e[:, n, D:2 * D], dis_out[:, bass.ds(r, 1)], u[:, r, :],
                                               ALU.mult, ALU.add).then_inc(sums_read, 1)
                spread(r, n % 2, 0)

            def head1(r, n):
                dve.wait_ge(hi_scaled, r + 1)
                nc.vector.scalar_tensor_tensor(summed[:, n % 2, :], ps_e[:, n, D:2 * D], w_down, summed[:, n % 2, :],
                                               ALU.mult, ALU.add).then_inc(sums_read, 1)
                dve.wait_ge(sums_read, r + (R + 1))
                nc.vector.scalar_tensor_tensor(u[:, r, :], summed[:, n % 2, :], 0.0, u[:, r, :],
                                               ALU.max, ALU.add).then_inc(relu_done, 1)
                spread(r, n % 2, R)

            def normalise(r, n, base, wait=True):
                q = n % 2
                dve.wait_ge(std_done, r + (base + 1))
                nc.vector.reciprocal(rstd[:, q:q + 1], std[:, q:q + 1]).then_inc(rstd_done, 1)
                dve.wait_ge(rstd_done, r + (base + 1))
                if base == 0 and wait:
                    dve.wait_ge(x1_turned, r - 3)
                    dve.wait_ge(x1_kept, r - 3)
                nc.vector.tensor_scalar(x1_now[:, n, :] if base == 0 else u[:, r, :], u[:, r, :],
                                        mean[q], rstd[:, q:q + 1], ALU.subtract,
                                        ALU.mult).then_inc(x1_done if base == 0 else out_done, 1)

            def xw_low(r, n):
                dve.wait_ge(xw_hi, r + 1)
                nc.vector.scalar_tensor_tensor(x_parts[:, r, D:2 * D], xw_ps[n % 2][:, 0:P], w_up,
                                               x_parts[:, r, 0:D], ALU.mult, ALU.subtract).then_inc(xw_lo, 1)

            def step(r, n, lag, more=True):
                dve.wait_ge(rows_done, r + 1)
                if lag >= G and more:
                    stage_block(r + 2, n % 2)
                head0(r, n)
                if lag >= 5:
                    xw_low(r - 5, (n + 3) % G)
                if lag >= 1:
                    normalise(r - 1, (n + 3) % G, 0, lag >= 5)
            for r in range(2 * G):
                step(r, r % G, r)
            with dve.Fori(2 * G, R - 2 * G + 1, G) as r:
                for n in range(G):
                    step(r + n, n, 5)
            for r in range(R - G, R):
                step(r, r % G, 5, r + 2 < R)
                if r + 2 >= R:
                    stage_block(G + r + 2 - R, r % 2)
            normalise(R - 1, (R - 1) % G, 0)
            for r in range(R - 5, R):
                xw_low(r, r % G)

            dve.wait_ge(x1_kept, R)

            def last_step(r, n, more=True, stage_next=True):
                dve.wait_ge(rows_done, r + (R + 1))
                if stage_next:
                    stage_block(r + 2, n % 2)
                head1(r, n)
                if more:
                    normalise(r - 1, (n + 3) % G, R)
            for r in range(G):
                last_step(r, r, r >= 1, False)
            with dve.Fori(G, R - 2 * G + 1, G) as r:
                for n in range(G):
                    last_step(r + n, n)
            for r in range(R - G, R):
                last_step(r, r % G, True, r + 2 < R)
            normalise(R - 1, (R - 1) % G, R)

        @block.tensor
        def _(pe):
            def keep_busy(n):
                for _ in range(n):
                    nc.tensor.matmul(ps_acc[:, 0:P], ident[:, :], ident[:, :], start=True, stop=True)

            pe.wait_ge(ident_done, 1)
            keep_busy(24)
            for g in range(H):
                if g >= 4:
                    keep_busy(3)
                pe.wait_ge(xn_done[g // 2], 1)
                if g >= 4:
                    pe.wait_ge(xnt_lo, g - 3)
                for n in range(TH):
                    t = TH * g + n
                    ins = nc.tensor.transpose(ps_e[:, g % 4, n * P:(n + 1) * P], scores[:, t * P:(t + 1) * P],
                                              ident[:, :])
                ins.then_inc(xnt_turned, 1)
                if g == 5:
                    pe.wait_ge(great_done, 1)
                    nc.tensor.transpose(ps_at[0:2, 0:P], great, ident[:, :]).then_inc(great_turned, 1)
                if g == 6:
                    pe.wait_ge(great_diag, 1)
                    nc.tensor.matmul(ps_at[:, 2 * P:2 * P + 2], ones2, pow2[0:2, :],
                                     start=True, stop=True).then_inc(great_spread, 1)

            def turn_adj(r, first=False):
                if first:
                    pe.wait_ge(scales_done, 1)
                else:
                    pe.wait_ge(adj_stored, r * C)
                pe.wait_ge(packed_done, r + 1)
                for n in range(CH // K // P):
                    ins = nc.tensor.transpose(ps_at[:, n * P:(n + 1) * P], packed_f[:, n * P:(n + 1) * P], ident[:, :])
                ins.then_inc(adj_turned, 1)

            def cosines(r, q, h, start=False):
                if start:
                    pe.wait_ge(xnt_lo, max(h + 1, 6) if h >= 2 else h + 1)
                if h == 0:
                    pe.wait_ge(signed, r + 1)
                if start and h in (4, 5):
                    pe.wait_ge(scores_done, h - 3)
                elif not start:
                    pe.wait_ge(scores_done, r * H + (h - 1))
                o = h * BANK
                for part, other in ((0, 0), (0, 1), (1, 0)):
                    ins = nc.tensor.matmul(score_bank(h, start), xn_signed[:, q, part, :], xn_parts[:, other, o:o + BANK],
                                           start=(part == 0 and other == 0), stop=(part == 1))
                ins.then_inc(s_done, 1)

            def turn_e(r, h, start=False):
                if h % 2 == 0:
                    pe.wait_ge(exp_done, r * C + (h // 2 + 1))
                if not (start and h < 4):
                    pe.wait_ge(e_lo, r * H + (h - 3))
                for n in range(TH):
                    t = TH * h + n
                    ins = nc.tensor.transpose(ps_e[:, h % 4, n * P:(n + 1) * P], scores[:, t * P:(t + 1) * P],
                                              ident[:, :])
                ins.then_inc(e_turned, 1)

            def attend(r, h, start=False):
                pe.wait_ge(e_lo, r * H + (h + 1))
                if h == 0 and not start:
                    pe.wait_ge(attn_read, r)
                if start and h % 2 == 0:
                    pe.wait_ge(x_lo, h // 2 + 1)
                for n in range(TH):
                    t = TH * h + n
                    nc.tensor.matmul(ps_acc[:, 0:2 * D], eT_parts[:, h % 4, 0, n * P:(n + 1) * P], x_parts[:, t, :],
                                     start=(t == 0), stop=(t == R - 1), skip_group_check=True)
                    ins = nc.tensor.matmul(ps_acc[:, 0:D], eT_parts[:, h % 4, 1, n * P:(n + 1) * P],
                                           x_parts[:, t, 0:D], start=False, stop=(t == R - 1), skip_group_check=True)
                ins.then_inc(attn_part, 1)

            def row(r, q, start=False, left=2):
                for h in range(H):
                    turn_e(r, h, start)
                    if h == 2:
                        turn_adj(r, start)
                    if h >= LAG:
                        attend(r, h - LAG, start)
                    elif h == 1 and not start:
                        attend(r - 1, H - 1)
                    if left and 1 <= h < H - 1:
                        cosines(r + 1, 1 - q, h + 1)
                for h in range(H - LAG, H - 1):
                    attend(r, h, start)
                    if left > 1:
                        cosines(r + 2, q, h - (H - LAG))

            keep_busy(4)
            for h in range(H):
                cosines(0, 0, h, start=True)
            cosines(1, 1, 0)
            cosines(1, 1, 1)
            row(0, 0, start=True)
            row(1, 1)
            with pe.Fori(2, R - 3, 2) as r:
                row(r, 0)
                row(r + 1, 1)
            row(R - 2, 0, left=1)
            row(R - 1, 1, left=0)
            attend(R - 1, H - 1)

            def add_tile(n, lhs, t, y):
                b, k = t // K, t % K
                return nc.tensor.matmul(ps_e[:, n, 0:2 * D], lhs[:, b, :, k], y[t],
                                        start=(t == 0), stop=(t == R - 1))

            def turn_x1(r, n):
                pe.wait_ge(x1_done, r + 1)
                nc.tensor.transpose(ps_s[:, n % 2, 0:P], x1_now[:, n, :], ident[:, :]).then_inc(x1_turned, 1)

            def x1_w(r, n):
                pe.wait_ge(x1t_done, r + 1)
                pe.wait_ge(xw_lo, r + 1)
                nc.tensor.matmul(xw_ps[n % 2][:, 0:P], x1t[:, n % 2, :], wts, start=True, stop=True).then_inc(xw_done, 1)

            def whole_row(r, n, y, layer):
                pe.wait_ge(staged, r + (layer * (R - G) - G + 1))
                pe.wait_ge(sums_read, r + (layer * R + 1 - G))
                for t in range(R):
                    ins = add_tile(n, stage8[n % 2], t, y)
                    if t == 0:
                        ins.wait_op(ident_done, 1, "sem-ge")
                    if layer == 0 and t == R // 2:
                        turn_x1(r - G, n)
                ins.then_inc(rows_done, 1)
                if layer == 0:
                    x1_w(r - G, n)

            y_tiles = [y_parts[:, t, :, :] for t in range(R)]
            xw_tiles = [x_parts[:, t, :] for t in range(R)]

            pe.wait_ge(e_lo, R * H)
            for r in range(G):
                for t in range(R):
                    if r == 0 and t % TC == 0:
                        pe.wait_ge(y_lo, t // TC + 1)
                    ins = add_tile(r, adjT8[r], t, y_tiles)
                ins.then_inc(rows_done, 1)
            pe.wait_ge(w_loaded, 32)
            with pe.Fori(G, R - G + 1, G) as r:
                for n in range(G):
                    whole_row(r + n, n, y_tiles, 0)

            def first_tiles(r, moments):
                for t in range(R - 2 * G):
                    if r == 0 and t == 0:
                        pe.wait_ge(xw_lo, R - 2 * G + 2)
                    if t == 0:
                        pe.wait_ge(sums_read, R - G + r + 1)
                    add_tile(r, adjT8[r], t, xw_tiles)
                    if t in moments:
                        work, n = moments[t]
                        work(R - G + n, n)

            def last_tiles(r):
                for t in range(R - 2 * G, R):
                    pe.wait_ge(xw_lo, t + 1 + 2)
                    ins = add_tile(r, adjT8[r], t, xw_tiles)
                ins.then_inc(rows_done, 1)
            first_tiles(0, {2: (turn_x1, 0), 16: (x1_w, 0), 18: (turn_x1, 1)})
            first_tiles(1, {2: (x1_w, 1), 4: (turn_x1, 2), 11: (x1_w, 2), 13: (turn_x1, 3), 20: (x1_w, 3)})
            last_tiles(0)
            last_tiles(1)
            for r in range(2, G):
                first_tiles(r, {})
                last_tiles(r)
            with pe.Fori(G, R - G + 1, G) as r:
                for n in range(G):
                    whole_row(r + n, n, xw_tiles, 1)


_INS = ["x", "adj", "L0_gnn_alpha", "L0_gnn_beta", "L1_gnn_weights"]


def kernel(**inputs):
    import numpy as _np
    import concourse.bacc as _bacc
    from concourse import mybir as _mybir
    from concourse.bass_utils import run_bass_kernel_spmd as _run

    nc = _bacc.Bacc("TRN2", target_bir_lowering=False, num_devices=1, dynamic_dma_scratch_size=1024)
    arrays, args = {}, []
    for name in _INS:
        a = _np.ascontiguousarray(inputs[name])
        arrays[f"in_{name}"] = a
        args.append(nc.dram_tensor(f"in_{name}", a.shape, _mybir.dt.from_np(a.dtype), kind="ExternalInput").ap())
    res = nc.dram_tensor("out_0", (4096, 128), _mybir.dt.float32, kind="ExternalOutput").ap()
    two_layer_gnn(nc, *args, res)
    r = _run(nc, [arrays], core_ids=[0])
    return r.results[0]["out_0"]
```
